# Optimizing a Trainium2 kernel written in Bass

```python
import numpy as np
import jax
import jax.numpy as jnp

def _softmax(x, axis=-1):
    return jax.nn.softmax(x, axis=axis)

def _gelu(x):
    return jax.nn.gelu(x, approximate=True)

def _silu(x):
    return jax.nn.silu(x)

def _sigmoid(x):
    return jax.nn.sigmoid(x)

def _layernorm(x, axis=-1, eps=1e-05):
    m = jnp.mean(x, axis=axis, keepdims=True)
    v = jnp.var(x, axis=axis, keepdims=True)
    return (x - m) / jnp.sqrt(v + eps)

def _scatter_add(tgt, idx, src, axis=0):
    return tgt.at[idx].add(src)

def _segment_sum(src, seg, n):
    return jax.ops.segment_sum(src, seg, n)
kernel_name = 'mk_gnn_resnorm_d1_gnn_r64_0eac73'

def setup_inputs(seed: int=0):
    np.random.seed(seed)
    _w = jnp.asarray

    def _rec_inputs():
        import jax
        import jax.numpy as jnp
        _gk = jax.random.key(seed)
        x = -0.000202 + 1 * jax.random.normal(jax.random.fold_in(_gk, 1), (100000, 128), jnp.float32)
        src = jax.random.randint(jax.random.fold_in(_gk, 2), (50000,), 0, 100000, jnp.int32)
        dst = jnp.minimum((100000 * jax.random.uniform(jax.random.fold_in(_gk, 3), (50000,)) ** 2.0).astype(jnp.int32), 99999)
        _o = jnp.argsort(dst, stable=True)
        src = src[_o]
        dst = dst[_o]
        return (x, src, dst)
    x, src, dst = _rec_inputs()

    def _L0_gnn_setup():
        import jax, jax.numpy as jnp
        import numpy as np
        N_NODES = 50000
        N_EDGES = 12500
        IN_CH = 128
        OUT_CH = 128
        key = jax.random.key(seed)
        k1, k2, k3, k4 = jax.random.split(key, 4)
        x = jax.random.normal(k1, (N_NODES, IN_CH), dtype=jnp.float32)
        edge_index = jax.random.randint(k2, (2, N_EDGES), 0, N_NODES, dtype=jnp.int64)
        W = jax.random.normal(k3, (OUT_CH, IN_CH), dtype=jnp.float32) / np.sqrt(IN_CH)
        b = jax.random.normal(k4, (OUT_CH,), dtype=jnp.float32) * 0.01
        agg_weight = jnp.ones((1,), dtype=jnp.float32)
        return {'x': x, 'edge_index': edge_index, 'W': W, 'b': b, 'agg_weight': agg_weight}
    _L0_gnn_all = _L0_gnn_setup()
    _L0_gnn_in = {k: v for k, v in _L0_gnn_all.items() if k in ('W', 'b', 'agg_weight')}
    del _L0_gnn_all
    return {'x': x, 'src': src, 'dst': dst, 'L0_gnn_W': _L0_gnn_in['W'], 'L0_gnn_b': _L0_gnn_in['b'], 'L0_gnn_agg_weight': _L0_gnn_in['agg_weight']}

def reference(x, src, dst, L0_gnn_W, L0_gnn_b, L0_gnn_agg_weight):
    import jax
    import jax.numpy as jnp

    def _L0_gnn_ref(x, edge_index, W, b, agg_weight):
        import jax, jax.numpy as jnp
        import numpy as np
        N_NODES = 50000
        N_EDGES = 12500
        IN_CH = 128
        OUT_CH = 128
        row, col = (edge_index[0], edge_index[1])
        messages = jnp.einsum('ei,oi->eo', x[col], W) + b
        out = jax.ops.segment_sum(messages * agg_weight, row, num_segments=x.shape[0])
        return out
    edge_index = jnp.stack([src, dst])
    x = _layernorm(x + _L0_gnn_ref(x, edge_index, L0_gnn_W, L0_gnn_b, L0_gnn_agg_weight), axis=-1)
    return x

_drawn_inputs = setup_inputs


def setup_inputs(seed=0):
    import zlib

    import numpy as np

    out = dict(_drawn_inputs(seed))
    spreads = {}
    factors = {'L0_gnn_b': 8.0}
    for name, (base, spread) in spreads.items():
        noise = np.random.default_rng([zlib.crc32(name.encode()), seed]).standard_normal(out[name].shape)
        drawn = base * np.exp(spread * noise) if base else spread * noise
        out[name] = jnp.asarray(drawn.astype(out[name].dtype))
    for name, factor in factors.items():
        out[name] = (out[name] * factor).astype(out[name].dtype)
    return out
```

```python
import concourse.bass as bass
from concourse import mybir
from contextlib import ExitStack


def gnn_resnorm_kernel(nc, x, src, dst, W, b, agg_weight, out):
    f32, i32 = mybir.dt.float32, mybir.dt.int32
    ALU, ACT, AX = mybir.AluOpType, mybir.ActivationFunctionType, mybir.AxisListType.X
    P = 128
    N, D = x.shape
    E = src.shape[0]
    C = -(-E // P)
    KB = -(-C // P)
    GN = 4 * P
    G = N // GN
    PL = (N - G * GN) // 4
    PAD = 1 << 17
    EPS = 1e-5

    ctx = ExitStack()
    with ctx:
        def sb(name, shape, dt=f32):
            return ctx.enter_context(nc.sbuf_tensor(name, shape, dt))

        def ps(name, shape, dt=f32):
            return ctx.enter_context(nc.psum_tensor(name, shape, dt))

        def sem(name):
            return ctx.enter_context(nc.semaphore(name))

        src_rows = sb("src_rows", [P, KB, P], i32)
        dst_rows = sb("dst_rows", [P, KB, P], i32)
        srcf_rows = sb("srcf_rows", [P, KB, P])
        dstf_rows = sb("dstf_rows", [P, KB, P])
        src_col = sb("src_col", [P, KB * P])
        dst_idx = sb("dst_idx", [P, KB * P], i32)
        src_idx = sb("src_idx", [P, KB * P], i32)
        ident = sb("ident", [P, P])
        ones = sb("ones", [P, P])
        earlier = sb("earlier", [P, P])
        w_sb = sb("w_sb", [P, P])
        wT = sb("wT", [P, P])
        b_bc = sb("b_bc", [P, D])
        baw = sb("baw", [P, D])
        aw = sb("aw", [P, 1])
        xg = sb("xg", [P, D])
        hg = sb("hg", [P, D])
        xgT = sb("xgT", [P, P])
        diag = sb("diag", [P, P])
        eq = sb("eq", [P, P])
        msg = sb("msg", [P, D])
        junk = sb("junk", [P, P])
        cnt = sb("cnt", [P, 1])
        skip = sb("skip", [P, 1])
        widx = sb("widx", [P, 1], i32)
        now_src = sb("now_src", [P, 1], i32)
        now_dst = sb("now_dst", [P, 1], i32)
        h = sb("h", [P, 4, D])
        sq = sb("sq", [P, 4, D])
        st = sb("st", [P, 4, 4])

        pA = ps("pA", [P, KB * P])
        pB = ps("pB", [P, KB * P])
        pT = ps("pT", [P, P])
        pM = ps("pM", [P, D])
        pR = ps("pR", [P, P])
        pC = ps("pC", [P, D])

        s_fill = sem("s_fill")
        s_edges = sem("s_edges")
        s_w = sem("s_w")
        s_const = sem("s_const")
        s_const1 = sem("s_const1")
        s_rows = sem("s_rows")
        s_cols = sem("s_cols")
        s_idx = sem("s_idx")
        s_seed = sem("s_seed")
        s_xg = sem("s_xg")
        s_hg = sem("s_hg")
        s_pT = sem("s_pT")
        s_xgT = sem("s_xgT")
        s_msg_ps = sem("s_msg_ps")
        s_eq = sem("s_eq")
        s_msg = sem("s_msg")
        s_comb = sem("s_comb")
        s_hnew = sem("s_hnew")
        s_now = sem("s_now")
        s_cnt = sem("s_cnt")
        s_scat = sem("s_scat")
        s_h = sem("s_h")
        s_dve = sem("s_dve")
        s_sq = sem("s_sq")
        s_var = sem("s_var")
        s_std = sem("s_std")
        s_norm = sem("s_norm")
        s_store = sem("s_store")

        block = ctx.enter_context(nc.Block())

        @block.sync
        def _(sp):
            sp.wait_ge(s_fill, 2)
            for rows, arr in ((src_rows, src), (dst_rows, dst)):
                full = E // (P * P)
                sp.dma_start(rows[:, 0:full, :], arr[0:full * P * P].rearrange("(k r p) -> r k p", r=P, p=P)
                             ).then_inc(s_edges, 16)
                r = (E - full * P * P) // P
                sp.dma_start(rows[0:r, full, :], arr[full * P * P:(full * P + r) * P].rearrange("(r p) -> r p", p=P)
                             ).then_inc(s_edges, 16)
                sp.dma_start(rows[r:r + 1, full, 0:E - (full * P + r) * P],
                             arr[(full * P + r) * P:E].rearrange("(r p) -> r p", r=1)).then_inc(s_edges, 16)
            sp.dma_start(w_sb[:], W).then_inc(s_w, 16)
            sp.dma_start(b_bc[:], b.rearrange("(o d) -> o d", o=1).broadcast_to([P, D])).then_inc(s_w, 16)
            sp.dma_start(aw[:], agg_weight.rearrange("(o d) -> o d", o=1).broadcast_to([P, 1])).then_inc(s_w, 16)
            sp.dma_start(out.rearrange("(a n) d -> a (n d)", a=16), x.rearrange("(a n) d -> a (n d)", a=16)
                         ).then_inc(s_seed, 16)
            sp.sem_inc(s_store, 16)
            sp.wait_ge(s_scat, 16 * C)
            with sp.Fori(0, G) as g:
                sp.wait_ge(s_store, g * 16 + 16)
                sp.dma_start(h[:], out[bass.ds(g * GN, GN), :].rearrange("(p j) d -> p j d", j=4)).then_inc(s_h, 16)
                sp.wait_ge(s_norm, g + 1)
                sp.dma_start(out[bass.ds(g * GN, GN), :].rearrange("(p j) d -> p j d", j=4), h[:]).then_inc(s_store, 16)
            sp.wait_ge(s_store, G * 16 + 16)
            sp.dma_start(h[0:PL], out[G * GN:N, :].rearrange("(p j) d -> p j d", j=4)).then_inc(s_h, 16)
            sp.wait_ge(s_norm, G + 1)
            sp.dma_start(out[G * GN:N, :].rearrange("(p j) d -> p j d", j=4), h[0:PL]).then_inc(s_store, 16)
            sp.wait_ge(s_store, G * 16 + 32)

        @block.gpsimd
        def _(pool):
            nc.gpsimd.memset(src_rows[:], PAD).then_inc(s_fill, 1)
            nc.gpsimd.memset(dst_rows[:], PAD).then_inc(s_fill, 1)
            nc.gpsimd.memset(ones[:], 1.0).then_inc(s_const1, 1)
            nc.gpsimd.memset(xg[:], 0.0).then_inc(s_const1, 1)
            nc.gpsimd.memset(hg[:], 0.0).then_inc(s_const1, 1)
            pool.wait_ge(s_const1, 3)
            nc.gpsimd.affine_select(out=ident[:], in_=ones[:], compare_op=ALU.is_equal, fill=0.0, base=0,
                                    pattern=[[-1, P]], channel_multiplier=1).then_inc(s_const, 1)
            nc.gpsimd.affine_select(out=earlier[:], in_=ones[:], compare_op=ALU.is_gt, fill=0.0, base=0,
                                    pattern=[[-1, P]], channel_multiplier=1).then_inc(s_const, 1)
            pool.wait_ge(s_idx, 1)
            last_node = pool.to_reg(N - 1)
            pool.wait_ge(s_seed, 16)
            with pool.Fori(0, C) as c:
                pool.wait_ge(s_now, 2 * c + 2)
                pool.nop(nofuse=True)
                nc.gpsimd.indirect_dma_start(
                    out=xg[:], out_offset=None, in_=x, in_offset=bass.IndirectOffsetOnAxis(ap=now_dst[:], axis=0),
                    bounds_check=last_node, oob_is_err=False).then_inc(s_xg, 16)
                nc.gpsimd.indirect_dma_start(
                    out=hg[:], out_offset=None, in_=out, in_offset=bass.IndirectOffsetOnAxis(ap=now_src[:], axis=0),
                    bounds_check=last_node, oob_is_err=False).then_inc(s_hg, 16)
                pool.wait_ge(s_hnew, c + 1)
                pool.nop(nofuse=True)
                nc.gpsimd.indirect_dma_start(
                    out=out, out_offset=bass.IndirectOffsetOnAxis(ap=widx[:], axis=0), in_=msg[:], in_offset=None,
                    bounds_check=last_node, oob_is_err=False).then_inc(s_scat, 16)
                pool.wait_ge(s_scat, c * 16 + 16)
                pool.nop(nofuse=True)


        @block.tensor
        def _(pe):
            pe.wait_ge(s_const, 1)
            pe.wait_ge(s_w, 48)
            nc.tensor.transpose(pT[:], w_sb[:], ident[:])
            pe.wait_ge(s_rows, 2)
            for rows, cols in ((srcf_rows, pA), (dstf_rows, pB)):
                for k in range(KB):
                    nc.tensor.transpose(cols[:, k * P:(k + 1) * P], rows[:, k, :], ident[:]).then_inc(s_cols, 1)
            pe.wait_ge(s_idx, 1)
            with pe.Fori(0, C) as c:
                pe.wait_ge(s_xg, 16 * c + 16)
                nc.tensor.transpose(pT[:], xg[:], ident[:]).then_inc(s_pT, 1)
                pe.wait_ge(s_xgT, 2 * c + 2)
                nc.tensor.matmul(pR[:], ones[:], diag[:], start=True, stop=True)
                nc.tensor.matmul(pM[:], xgT[:], wT[:], start=True, stop=True).then_inc(s_msg_ps, 1)
                pe.wait_ge(s_msg, c + 1)
                pe.wait_ge(s_eq, c + 1)
                nc.tensor.matmul(pC[:], eq[:], msg[:], start=True, stop=True).then_inc(s_comb, 1)

        @block.vector
        def _(dve):
            dve.wait_ge(s_edges, 96)
            nc.vector.tensor_copy(srcf_rows[:], src_rows[:]).then_inc(s_rows, 1)
            nc.vector.tensor_copy(dstf_rows[:], dst_rows[:]).then_inc(s_rows, 1)
            dve.wait_ge(s_w, 48)
            nc.vector.tensor_scalar(baw[:], b_bc[:], aw[:], None, ALU.mult).then_inc(s_dve, 1)
            dve.wait_ge(s_cols, 2 * KB)
            nc.vector.tensor_copy(wT[:], pT[:]).then_inc(s_dve, 1)
            nc.vector.tensor_copy(src_col[:], pA[:]).then_inc(s_dve, 1)
            nc.vector.tensor_copy(src_idx[:], pA[:]).then_inc(s_dve, 1)
            nc.vector.tensor_copy(dst_idx[:], pB[:]).then_inc(s_dve, 1)
            dve.wait_ge(s_dve, 5)
            dve.wait_ge(s_const, 2)
            nc.vector.memset(junk[:], 0.0).then_inc(s_idx, 1)
            with dve.Fori(0, C) as c:
                mine = src_col[:, bass.ds(c, 1)]
                nc.vector.tensor_copy(now_dst[:], dst_idx[:, bass.ds(c, 1)]).then_inc(s_now, 1)
                nc.vector.tensor_copy(now_src[:], src_idx[:, bass.ds(c, 1)]).then_inc(s_now, 1)
                dve.wait_ge(s_pT, c + 1)
                nc.vector.tensor_copy(xgT[:], pT[:]).then_inc(s_xgT, 1)
                nc.vector.tensor_scalar(diag[:], ident[:], mine, None, ALU.mult).then_inc(s_xgT, 1)
                dve.wait_ge(s_msg_ps, c + 1)
                nc.vector.scalar_tensor_tensor(msg[:], pM[:], aw[:], baw[:], ALU.mult, ALU.add).then_inc(s_msg, 1)
                nc.vector.tensor_scalar(eq[:], pR[:], mine, None, ALU.is_equal).then_inc(s_eq, 1)
                dve.wait_ge(s_eq, c + 1)
                nc.vector.scalar_tensor_tensor(junk[:], eq[:], 1.0, earlier[:], ALU.mult, ALU.mult,
                                               accum_out=cnt[:]).then_inc(s_cnt, 1)
                dve.wait_ge(s_cnt, 3 * c + 1)
                nc.vector.tensor_scalar(skip[:], cnt[:], 1.0, float(1 << 20), ALU.min, ALU.mult).then_inc(s_cnt, 1)
                dve.wait_ge(s_cnt, 3 * c + 2)
                nc.vector.tensor_tensor(widx[:], skip[:], mine, ALU.add).then_inc(s_cnt, 1)
                dve.wait_ge(s_comb, c + 1)
                dve.wait_ge(s_hg, 16 * c + 16)
                dve.wait_ge(s_cnt, 3 * c + 3)
                nc.vector.tensor_tensor(msg[:], pC[:], hg[:], ALU.add).then_inc(s_hnew, 1)

            def layernorm(p, g):
                dve.wait_ge(s_h, 16 * g + 16)
                hh, qq = h[0:p], sq[0:p]
                nc.vector.tensor_reduce(st[0:p, 0, :], hh, AX, ALU.add).then_inc(s_var, 1)
                dve.wait_ge(s_var, 5 * g + 1)
                nc.vector.tensor_scalar(st[0:p, 1, :], st[0:p, 0, :], 1.0 / D, None, ALU.mult).then_inc(s_var, 1)
                dve.wait_ge(s_var, 5 * g + 2)
                nc.vector.tensor_tensor(hh, hh, st[0:p, 1, :].unsqueeze(2).broadcast_to([p, 4, D]), ALU.subtract
                                        ).then_inc(s_var, 1)
                dve.wait_ge(s_var, 5 * g + 3)
                nc.vector.tensor_tensor(qq, hh, hh, ALU.mult).then_inc(s_sq, 1)
                dve.wait_ge(s_sq, g + 1)
                nc.vector.tensor_reduce(st[0:p, 2, :], qq, AX, ALU.add).then_inc(s_var, 1)
                dve.wait_ge(s_var, 5 * g + 4)
                nc.vector.tensor_scalar(st[0:p, 0, :], st[0:p, 2, :], 1.0 / D, EPS, ALU.mult, ALU.add).then_inc(s_var, 1)
                dve.wait_ge(s_std, 2 * g + 1)
                nc.vector.reciprocal(st[0:p, 2, :], st[0:p, 3, :]).then_inc(s_std, 1)
                dve.wait_ge(s_std, 2 * g + 2)
                nc.vector.tensor_tensor(hh, hh, st[0:p, 2, :].unsqueeze(2).broadcast_to([p, 4, D]), ALU.mult
                                        ).then_inc(s_norm, 1)

            with dve.Fori(0, G) as g:
                layernorm(P, g)
            layernorm(PL, G)

        @block.scalar
        def _(act):
            def root(p, g):
                act.wait_ge(s_var, 5 * g + 5)
                nc.scalar.activation(st[0:p, 3, :], st[0:p, 0, :], ACT.Sqrt).then_inc(s_std, 1)

            with act.Fori(0, G) as g:
                root(P, g)
            root(PL, G)


_INS = ['x', 'src', 'dst', 'L0_gnn_W', 'L0_gnn_b', 'L0_gnn_agg_weight']


def kernel(**inputs):
    import numpy as _np
    import concourse.bacc as _bacc
    from concourse import mybir as _mybir
    from concourse.bass_utils import run_bass_kernel_spmd as _run

    nc = _bacc.Bacc("TRN2", target_bir_lowering=False, num_devices=1)
    arrays, args = {}, []
    for name in _INS:
        a = _np.ascontiguousarray(inputs[name])
        arrays[f"in_{name}"] = a
        args.append(nc.dram_tensor(f"in_{name}", a.shape, _mybir.dt.from_np(a.dtype), kind="ExternalInput").ap())
    shape = inputs['x'].shape
    args.append(nc.dram_tensor("out_0", shape, _mybir.dt.float32, kind="ExternalOutput").ap())
    gnn_resnorm_kernel(nc, *args)
    r = _run(nc, [arrays], core_ids=[0])
    return r.results[0]["out_0"]
```

```python
import concourse.bass as bass
from concourse import mybir
from contextlib import ExitStack



def gnn_resnorm_kernel(nc, x, src, dst, W, b, agg_weight, t_scratch, hi_scratch, out, most=128):
    f32, i32 = mybir.dt.float32, mybir.dt.int32
    bf16, f16 = mybir.dt.bfloat16, mybir.dt.float16
    ALU, ACT, AX = mybir.AluOpType, mybir.ActivationFunctionType, mybir.AxisListType.X
    P = 128
    N, D = x.shape
    E = src.shape[0]
    GN = 4 * P
    G = N // GN
    PL = (N - G * GN) // 4
    GA = G + 1
    NB = 3 * GA
    NH = NB // 2
    LO = 32
    HI = -(-NB // LO) + 1
    C = -(-E // P)
    BC = 16
    B = -(-C // BC)
    CA = B * BC
    KB = 4
    PAD = 1 << 17
    FULL = 1 << 30
    R = 4
    EPS = 1e-5
    assert CA <= KB * P and (B - 1) % 2 == 0 and GA % R == 0 and 3 * GN // 512 == 3

    ctx = ExitStack()
    with ctx:
        def sb(name, shape, dt=f32):
            return ctx.enter_context(nc.sbuf_tensor(name, shape, dt))

        def sem(name):
            return ctx.enter_context(nc.semaphore(name))

        def at_least(eng, s, count):
            if not isinstance(count, int) or count > 0:
                eng.wait_ge(s, count)

        ones = sb("ones", [P, P])
        ident = sb("ident", [P, P])
        earlier = sb("earlier", [P, P])
        earlier16 = sb("earlier16", [P, P], f16)
        iota_nb = sb("iota_nb", [P, NB], f16)
        iota_win = sb("iota_win", [P, 2 * P])
        iota_winh = sb("iota_winh", [P, 2 * P], f16)
        iota_lo = sb("iota_lo", [P, LO])
        part = sb("part", [P, 1])
        ones_scan = sb("ones_scan", [HI, CA], bf16)
        ones3 = sb("ones3", [P, 3], bf16)
        eps = sb("eps", [P, 1])
        w_sb = sb("w_sb", [P, P])
        wT = sb("wT", [P, P])
        b_bc = sb("b_bc", [P, D])
        aw = sb("aw", [P, 1])
        b_res = sb("b_res", [3, D])
        b_parts = sb("b_parts", [3, 3, D], bf16)
        b_acc = sb("b_acc", [3, D])
        b3 = sb("b3", [3, D], bf16)
        src_rows = sb("src_rows", [P, KB, P], i32)
        dst_rows = sb("dst_rows", [P, KB, P], i32)
        e0 = sb("e0", [P, KB, P], i32)
        e1 = sb("e1", [P, KB, P], i32)
        e2 = sb("e2", [P, KB, P], i32)
        pos = sb("pos", [P, KB, P], i32)
        third = sb("third", [P, KB, P], i32)
        bucket = sb("bucket", [P, KB, P], i32)
        word1 = sb("word1", [P, KB, P], i32)
        word2 = sb("word2", [P, KB, P], i32)
        t16_rows = sb("t16_rows", [P, KB, P], f16)
        hi_rows = sb("hi_rows", [P, KB, P], bf16)
        turn = sb("turn", [P, 5, KB, P])
        t_col = sb("t_col", [P, KB * P])
        hi_col = sb("hi_col", [P, KB * P])
        lo_col = sb("lo_col", [P, KB * P])
        w1_col = sb("w1_col", [P, KB * P])
        w2_col = sb("w2_col", [P, KB * P])
        src_col = sb("src_col", [P, KB * P])
        src_idx = sb("src_idx", [P, KB * P], i32)
        dst_idx = sb("dst_idx", [P, KB * P], i32)
        oh_lo = sb("oh_lo", [P, CA, LO], bf16)
        oh_hi = sb("oh_hi", [P, CA, HI], bf16)
        hist_all = sb("hist_all", [P, CA, LO], bf16)
        hist = hist_all[0:HI]
        before = sb("before", [HI, CA + 1, LO], bf16)
        most_hi = sb("most_hi", [HI, 1])
        most_all = sb("most_all", [1, 1])
        over = sb("over", [1, 1], i32)
        t_row = sb("t_row", [P, 2, BC * P], f16)
        hi_row = sb("hi_row", [HI, 2, BC * P], bf16)
        oh_hiT = sb("oh_hiT", [HI, 2, BC * P], bf16)
        t_now = sb("t_now", [P, 2, BC])
        w1_now = sb("w1_now", [P, 2, BC])
        w2_now = sb("w2_now", [P, 2, BC])
        junk16 = sb("junk16", [P, 4, P], f16)
        own = sb("own", [P, BC, LO], bf16)
        base = sb("base", [P, BC])
        within = sb("within", [P, 2, BC])
        slot = sb("slot", [P, 2, BC])
        oh_t = sb("oh_t", [P, 4, NB], bf16)
        oh_s1 = sb("oh_s1", [P, 4, P], bf16)
        oh_s2 = sb("oh_s2", [P, 8, P], bf16)
        turned = turn[:].rearrange("p a k r -> p (a k r)")
        tab1, tab2 = turned[:, 0:NB], turned[:, NB:2 * NB]
        emp, low5 = (turned[:, i * NB:(i + 1) * NB].bitcast(i32) for i in (2, 3))
        tabi = sb("tabi", [P, NB], i32)
        node_idx = sb("node_idx", [P, NB + 3 * R], i32)
        tabq = sb("tabq", [P, NB], i32)
        q_win = sb("q_win", [P, NB])
        now_idx = sb("now_idx", [P, R, 3], i32)
        q_now = sb("q_now", [P, R, 3])
        late1 = oh_lo[:].rearrange("p c l -> p (c l)").bitcast(f32)
        late2 = hist_all[:].rearrange("p c l -> p (c l)").bitcast(f32)
        SW, XW, TW = R * 3 * 2 * P, R * 3 * D, R * 4 * D
        sel = late1[:, 0:SW].rearrange("p (r k n) -> p r k n", r=R, k=3)
        selh = late1[:, SW:SW + SW // 2].bitcast(bf16).rearrange("p (r k n) -> p r k n", r=R, k=3)
        xg = late2[:, 0:XW].rearrange("p (r k d) -> p r k d", r=R, k=3)
        xt = late2[:, XW:XW + TW].rearrange("p (r j d) -> p r j d", r=R, j=4)
        h = late2[:, XW + TW:XW + 2 * TW].rearrange("p (r j d) -> p r j d", r=R, j=4)
        aggT = sb("aggT", [P, 2, GN])
        deg = sb("deg", [3, 2, GN], bf16)
        sq = sb("sq", [P, 4, D])
        hsum = sb("hsum", [P, R, 4])
        nmean = sb("nmean", [P, R, 4])
        vsum = sb("vsum", [P, R, 4])
        std = sb("std", [P, R, 4])
        rstd = sb("rstd", [P, R, 4])
        baw = sb("baw", [P, D])
        xg1 = sb("xg1", [P, D])
        hg = sb("hg", [P, D])
        xgT = sb("xgT", [P, P])
        diag = sb("diag", [P, P])
        eq = sb("eq", [P, P])
        msg = sb("msg", [P, D])
        junk = sb("junk", [P, P])
        cnt = sb("cnt", [P, 1])
        skip = sb("skip", [P, 1])
        widx = sb("widx", [P, 1], i32)
        now_src = sb("now_src", [P, 1], i32)
        now_dst = sb("now_dst", [P, 1], i32)
        st = sb("st", [P, 4, 4])

        bank = [ctx.enter_context(nc.psum_tensor(f"bank{i}", [P, 512], f32)) for i in range(8)]
        SORT = bank[4:6]
        AGG, OUT, DEG = bank[0:2], bank[2:4], bank[4:6]
        pT, pM, pR, pC = (bank[i][:, 0:P] for i in range(4))

        s_fill = sem("s_fill")
        s_const = sem("s_const")
        s_made = sem("s_made")
        s_edges = sem("s_edges")
        s_w = sem("s_w")
        s_bp = sem("s_bp")
        s_rows = sem("s_rows")
        s_cols = sem("s_cols")
        s_cvt = sem("s_cvt")
        s_scratch = sem("s_scratch")
        s_ohk = sem("s_ohk")
        s_hist = sem("s_hist")
        s_histc = sem("s_histc")
        s_zero = sem("s_zero")
        s_before = sem("s_before")
        s_mx = sem("s_mx")
        s_mxT = sem("s_mxT")
        s_over = sem("s_over")
        s_trow = [sem(f"s_trow{i}") for i in range(2)]
        s_hrow = [sem(f"s_hrow{i}") for i in range(2)]
        s_hiT = sem("s_hiT")
        s_now = sem("s_now")
        s_within = sem("s_within")
        s_q = sem("s_q")
        s_own = sem("s_own")
        s_base = sem("s_base")
        s_slot = sem("s_slot")
        s_oh = sem("s_oh")
        s_oh2 = sem("s_oh2")
        s_place = sem("s_place")
        s_clean = sem("s_clean")
        s_dec = sem("s_dec")
        s_idx = sem("s_idx")
        s_qn = sem("s_qn")
        s_g = [sem(f"s_g{i}") for i in range(R)]
        s_x = [sem(f"s_x{i}") for i in range(R)]
        s_st = [sem(f"s_st{i}") for i in range(R)]
        s_sel = sem("s_sel")
        s_agg = sem("s_agg")
        s_aggc = sem("s_aggc")
        s_out = sem("s_out")
        s_h = sem("s_h")
        s_mean = sem("s_mean")
        s_var = sem("s_var")
        s_std = sem("s_std")
        s_rstd = sem("s_rstd")
        s_y = sem("s_y")
        z_seed = sem("z_seed")
        z_init = sem("z_init")
        z_xg = sem("z_xg")
        z_hg = sem("z_hg")
        z_pT = sem("z_pT")
        z_xgT = sem("z_xgT")
        z_msg_ps = sem("z_msg_ps")
        z_eq = sem("z_eq")
        z_msg = sem("z_msg")
        z_comb = sem("z_comb")
        z_hnew = sem("z_hnew")
        z_now = sem("z_now")
        z_cnt = sem("z_cnt")
        z_scat = sem("z_scat")
        z_h = sem("z_h")
        z_sq = sem("z_sq")
        z_var = sem("z_var")
        z_std = sem("z_std")
        z_norm = sem("z_norm")
        z_store = sem("z_store")

        def batches(eng, step):
            for k in range(3):
                step(k, k % 2, k // 2)
            with eng.Fori(1, (B - 1) // 2) as i:
                step(i * 2 + 1, 1, i)
                step(i * 2 + 2, 0, i + 1)

        def rounds(eng, stages):
            def static(i):
                for stage, lag in stages:
                    if 0 <= i - lag < GA:
                        stage(i - lag, (i - lag) % R, (i - lag) // R)

            for i in range(2 * R):
                static(i)
            with eng.Fori(2, GA // R - 1) as r:
                for u in range(R):
                    for stage, lag in stages:
                        stage(r * R + (u - lag), (u - lag) % R, r + (u - lag) // R)
            for i in range(GA - R, GA + max(lag for _, lag in stages)):
                static(i)

        block = ctx.enter_context(nc.Block())

        @block.sync
        def _(sp):
            sp.wait_ge(s_fill, 2)
            full = E // (P * P)
            r = (E - full * P * P) // P
            done = (full * P + r) * P
            for rows, arr in ((src_rows, src), (dst_rows, dst)):
                sp.dma_start(rows[:, 0:full, :], arr[0:full * P * P].rearrange("(k r p) -> r k p", r=P, p=P)
                             ).then_inc(s_edges, 16)
                sp.dma_start(rows[0:r, full, :], arr[full * P * P:done].rearrange("(r p) -> r p", p=P)
                             ).then_inc(s_edges, 16)
                sp.dma_start(rows[r:r + 1, full, 0:E - done], arr[done:E].rearrange("(r p) -> r p", r=1)
                             ).then_inc(s_edges, 16)
            sp.dma_start(w_sb[:], W).then_inc(s_w, 16)
            sp.dma_start(b_bc[:], b.rearrange("(o d) -> o d", o=1).broadcast_to([P, D])).then_inc(s_w, 16)
            sp.dma_start(aw[:], agg_weight.rearrange("(o d) -> o d", o=1).broadcast_to([P, 1])).then_inc(s_w, 16)
            sp.wait_ge(s_rows, 2)
            sp.dma_start(t_scratch.rearrange("(k r p) -> r k p", r=P, p=P), t16_rows[:]).then_inc(s_scratch, 16)
            sp.dma_start(hi_scratch.rearrange("(k r p) -> r k p", r=P, p=P), hi_rows[:]).then_inc(s_scratch, 16)
            sp.wait_ge(s_scratch, 32)

            def load_rows(k, q, n):
                at_least(sp, s_hiT, k - 1)
                sp.dma_start(hi_row[:, q], hi_scratch[bass.ds(k * (BC * P), BC * P)].rearrange(
                    "(o n) -> o n", o=1).broadcast_to([HI, BC * P])).then_inc(s_hrow[q], 16)
                at_least(sp, s_within, k * BC - BC)
                sp.dma_start(t_row[:, q], t_scratch[bass.ds(k * (BC * P), BC * P)].rearrange(
                    "(o n) -> o n", o=1).broadcast_to([P, BC * P])).then_inc(s_trow[q], 16)

            load_rows(0, 0, 0)
            load_rows(1, 1, 0)
            with sp.Fori(1, (B - 1) // 2) as i:
                load_rows(i * 2, 0, i)
                load_rows(i * 2 + 1, 1, i)
            load_rows(B - 1, 0, (B - 1) // 2)

            sp.wait_ge(s_over, 1)
            flag = sp.value_load(over[0:1, 0:1], min_val=0, max_val=1)
            with sp.If(flag):
                sp.dma_start(out.rearrange("(a n) d -> a (n d)", a=16), x.rearrange("(a n) d -> a (n d)", a=16)
                             ).then_inc(z_seed, 16)
                sp.wait_ge(z_scat, 16 * C)
                sp.sem_inc(z_store, 16)

                def pass_group(g, rows, p):
                    sp.wait_ge(z_store, g * 16 + 16)
                    sp.dma_start(h[0:p, 0], rows).then_inc(z_h, 16)
                    sp.wait_ge(z_norm, g + 1)
                    sp.dma_start(rows, h[0:p, 0]).then_inc(z_store, 16)

                with sp.Fori(0, G) as g:
                    pass_group(g, out[bass.ds(g * GN, GN), :].rearrange("(p j) d -> p j d", j=4), P)
                pass_group(G, out[G * GN:N, :].rearrange("(p j) d -> p j d", j=4), PL)
                sp.wait_ge(z_store, G * 16 + 32)
            with sp.Else():
                sp.wait_ge(s_clean, 2)

                def load(g, u, n):
                    at_least(sp, s_h, 4 * g - 4 * R + 4)
                    if isinstance(g, int) and g == G:
                        sp.dma_start(xt[0:PL, u], x[G * GN:N, :].rearrange("(p j) d -> p j d", j=4)).then_inc(s_x[u], 16)
                    else:
                        sp.dma_start(xt[:, u], x[bass.ds(g * GN, GN), :].rearrange("(p j) d -> p j d", j=4)
                                     ).then_inc(s_x[u], 16)

                def store(g, u, n):
                    sp.wait_ge(s_y, 4 * g + 4)
                    if isinstance(g, int) and g == G:
                        sp.dma_start(out[G * GN:N, :].rearrange("(p j) d -> p j d", j=4), h[0:PL, u]).then_inc(s_st[u], 16)
                    else:
                        sp.dma_start(out[bass.ds(g * GN, GN), :].rearrange("(p j) d -> p j d", j=4), h[:, u]
                                     ).then_inc(s_st[u], 16)

                rounds(sp, [(load, 0), (store, 4)])
                for u in range(R):
                    sp.wait_ge(s_st[u], 16 * (GA // R))

        @block.gpsimd
        def _(pool):
            nc.gpsimd.memset(src_rows[:], PAD).then_inc(s_fill, 1)
            nc.gpsimd.memset(dst_rows[:], PAD).then_inc(s_fill, 1)
            nc.gpsimd.memset(ones[:], 1.0).then_inc(s_made, 1)
            nc.gpsimd.iota(iota_lo[:], [[1, LO]], base=0, channel_multiplier=0,
                           allow_small_or_imprecise_dtypes=True).then_inc(s_const, 1)
            nc.gpsimd.iota(part[:], [[0, 1]], base=0, channel_multiplier=1,
                           allow_small_or_imprecise_dtypes=True).then_inc(s_const, 1)
            pool.wait_ge(s_made, 1)
            nc.gpsimd.affine_select(out=ident[:], in_=ones[:], compare_op=ALU.is_equal, fill=0.0, base=0,
                                    pattern=[[-1, P]], channel_multiplier=1).then_inc(s_const, 1)
            nc.gpsimd.affine_select(out=earlier[:], in_=ones[:], compare_op=ALU.is_gt, fill=0.0, base=0,
                                    pattern=[[-1, P]], channel_multiplier=1).then_inc(s_const, 1)
            nc.gpsimd.iota(iota_nb[:], [[1, NB]], base=0, channel_multiplier=0,
                           allow_small_or_imprecise_dtypes=True).then_inc(s_const, 1)
            nc.gpsimd.iota(iota_win[:], [[1, 2 * P]], base=0, channel_multiplier=0,
                           allow_small_or_imprecise_dtypes=True).then_inc(s_const, 1)
            nc.gpsimd.iota(iota_winh[:], [[1, 2 * P]], base=0, channel_multiplier=0,
                           allow_small_or_imprecise_dtypes=True).then_inc(s_const, 1)
            nc.gpsimd.memset(eps[:], EPS).then_inc(s_const, 1)
            nc.gpsimd.memset(ones3[:], 1.0).then_inc(s_const, 1)
            nc.gpsimd.memset(ones_scan[:], 1.0).then_inc(s_const, 1)
            nc.gpsimd.memset(xg1[:], 0.0).then_inc(z_init, 1)
            nc.gpsimd.memset(hg[:], 0.0).then_inc(z_init, 1)
            pool.wait_ge(s_const, 10)

            def one_hots(k, q, n):
                pool.wait_ge(s_hrow[q], 16 * n + 16)
                at_least(pool, s_q, k - 1)
                pool.nop(nofuse=True)
                nc.gpsimd.tensor_scalar(oh_hiT[:, q], hi_row[:, q], part[0:HI], None, ALU.is_equal).then_inc(s_hiT, 1)
                pool.wait_ge(s_slot, k + 1)
                for i in range(BC):
                    if i % 4 == 0:
                        at_least(pool, s_place, k * BC + (i - 4))
                        pool.nop(nofuse=True)
                    nc.gpsimd.tensor_scalar(oh_s2[:, i % 8], iota_nb[:, 0:P], slot[:, q, i:i + 1], w2_now[:, q, i:i + 1],
                                            ALU.is_equal, ALU.mult).then_inc(s_oh2, 1)

            batches(pool, one_hots)

            pool.wait_ge(s_over, 1)
            flag = pool.value_load(over[0:1, 0:1], min_val=0, max_val=1)
            last_node = pool.to_reg(N - 1)
            with pool.If(flag):
                pool.wait_ge(z_seed, 16)
                pool.wait_ge(z_init, 2)
                with pool.Fori(0, C) as c:
                    pool.wait_ge(z_now, 2 * c + 2)
                    pool.nop(nofuse=True)
                    nc.gpsimd.indirect_dma_start(
                        out=xg1[:], out_offset=None, in_=x, in_offset=bass.IndirectOffsetOnAxis(ap=now_dst[:], axis=0),
                        bounds_check=last_node, oob_is_err=False).then_inc(z_xg, 16)
                    nc.gpsimd.indirect_dma_start(
                        out=hg[:], out_offset=None, in_=out, in_offset=bass.IndirectOffsetOnAxis(ap=now_src[:], axis=0),
                        bounds_check=last_node, oob_is_err=False).then_inc(z_hg, 16)
                    pool.wait_ge(z_hnew, c + 1)
                    pool.nop(nofuse=True)
                    nc.gpsimd.indirect_dma_start(
                        out=out, out_offset=bass.IndirectOffsetOnAxis(ap=widx[:], axis=0), in_=msg[:], in_offset=None,
                        bounds_check=last_node, oob_is_err=False).then_inc(z_scat, 16)
                    pool.wait_ge(z_scat, c * 16 + 16)
                    pool.nop(nofuse=True)
            with pool.Else():
                pool.wait_ge(s_mx, 1)
                nc.gpsimd.memset(xt, 0.0).then_inc(s_clean, 1)
                nc.gpsimd.memset(xg, 0.0).then_inc(s_clean, 1)
                pool.wait_ge(s_clean, 2)

                def gather(g, u, n):
                    pool.wait_ge(s_idx, g + 1)
                    pool.nop(nofuse=True)
                    for k in range(3):
                        nc.gpsimd.indirect_dma_start(
                            out=xg[:, u, k], out_offset=None, in_=x,
                            in_offset=bass.IndirectOffsetOnAxis(ap=now_idx[:, u, k:k + 1], axis=0),
                            bounds_check=last_node, oob_is_err=False).then_inc(s_g[u], 16)

                rounds(pool, [(gather, 0)])

        @block.tensor
        def _(pe):
            pe.wait_ge(s_const, 4)
            pe.wait_ge(s_w, 48)
            nc.tensor.transpose(bank[7][:, 0:P], w_sb[:], ident[:]).then_inc(s_cols, 1)
            pe.wait_ge(s_rows, 8)
            for j, rows in enumerate((turn[:, 0], turn[:, 1], turn[:, 2], word1[:].bitcast(f32), turn[:, 3],
                                      turn[:, 4], word2[:].bitcast(f32))):
                for k in range(KB):
                    last = nc.tensor.transpose(bank[j][:, k * P:(k + 1) * P], rows[:, k, :], ident[:])
                last.then_inc(s_cols, 1)
            pe.wait_ge(s_cvt, 9)

            def histogram(k, q, n):
                pe.wait_ge(s_ohk, 2 * k + 2)
                at_least(pe, s_histc, k - 1)
                for i in range(BC):
                    last = nc.tensor.matmul(SORT[q][0:HI, i * LO:(i + 1) * LO], oh_hi[:, bass.ds(k * BC + i, 1)].rearrange("p o h -> p (o h)"),
                                            oh_lo[:, bass.ds(k * BC + i, 1)].rearrange("p o h -> p (o h)"), start=True, stop=True)
                last.then_inc(s_hist, 1)

            batches(pe, histogram)
            pe.wait_ge(s_mx, 1)
            nc.tensor.transpose(bank[7][0:1, 0:HI], most_hi[:], ident[0:HI, 0:HI]).then_inc(s_mxT, 1)
            pe.wait_ge(s_histc, B)

            def place(k, q, n):
                pe.wait_ge(s_hiT, k + 1)
                at_least(pe, s_own, k - 1)
                for i in range(BC):
                    last = nc.tensor.matmul(SORT[q][:, i * LO:(i + 1) * LO], oh_hiT[:, q, i * P:(i + 1) * P],
                                            before[:, bass.ds(k * BC + i, 1)].rearrange("p o h -> p (o h)"), start=True, stop=True)
                last.then_inc(s_q, 1)
                for i in range(BC):
                    pe.wait_ge(s_oh, k * (2 * BC) + (2 * i + 2))
                    pe.wait_ge(s_oh2, k * BC + (i + 1))
                    first = isinstance(k, int) and k == 0 and i == 0
                    for w, hot in ((0, oh_s1[:, i % 4]), (1, oh_s2[:, i % 8])):
                        for half in range(2):
                            last = nc.tensor.matmul(bank[2 * w + half][:, 0:NH], hot,
                                                    oh_t[:, i % 4, half * NH:(half + 1) * NH], start=first, stop=False,
                                                    skip_group_check=True)
                    last.then_inc(s_place, 1)

            batches(pe, place)

            pe.wait_ge(s_over, 1)
            flag = pe.value_load(over[0:1, 0:1], min_val=0, max_val=1)
            with pe.If(flag):
                pe.wait_ge(s_dec, 4)
                with pe.Fori(0, C) as c:
                    pe.wait_ge(z_xg, 16 * c + 16)
                    nc.tensor.transpose(pT, xg1[:], ident[:]).then_inc(z_pT, 1)
                    pe.wait_ge(z_xgT, 2 * c + 2)
                    nc.tensor.matmul(pR, ones[:], diag[:], start=True, stop=True)
                    nc.tensor.matmul(pM, xgT[:], wT[:], start=True, stop=True).then_inc(z_msg_ps, 1)
                    pe.wait_ge(z_msg, c + 1)
                    pe.wait_ge(z_eq, c + 1)
                    nc.tensor.matmul(pC, eq[:], msg[:], start=True, stop=True).then_inc(z_comb, 1)
            with pe.Else():
                pe.wait_ge(s_dec, 4)

                def aggregate(g, u, n):
                    pe.wait_ge(s_g[u], 48 * n + 48)
                    pe.wait_ge(s_sel, 6 * g + 6)
                    at_least(pe, s_aggc, 2 * g - 2)
                    q = u % 2
                    for k in range(3):
                        nc.tensor.matmul(AGG[q][:, k * P:(k + 2) * P], xg[:, u, k], sel[:, u, k],
                                         start=(k == 0), stop=(k == 2), skip_group_check=True)
                    for k in range(3):
                        last = nc.tensor.matmul(DEG[q][0:3, k * P:(k + 2) * P], ones3[:], selh[:, u, k],
                                                start=(k == 0), stop=(k == 2), skip_group_check=True)
                    last.then_inc(s_agg, 1)

                def project(g, u, n):
                    pe.wait_ge(s_aggc, 2 * g + 2)
                    at_least(pe, s_h, 4 * g - 4)
                    q = u % 2
                    for j in range(4):
                        nodes = slice(j * P, (j + 1) * P)
                        nc.tensor.matmul(OUT[q][:, nodes], aggT[:, q, nodes], wT[:], start=(j == 0), stop=False,
                                         skip_group_check=True)
                        last = nc.tensor.matmul(OUT[q][:, nodes], deg[:, q, nodes], b3[:], start=False, stop=True,
                                                skip_group_check=True)
                    last.then_inc(s_out, 1)

                rounds(pe, [(aggregate, 2), (project, 3)])

        @block.vector
        def _(dve):
            step_no = [0]

            def after(ins):
                step_no[0] += 1
                ins.then_inc(s_bp, 1)
                dve.wait_ge(s_bp, step_no[0])

            V = nc.vector
            LSR, LSL, AND, OR, XOR = (ALU.logical_shift_right, ALU.logical_shift_left, ALU.bitwise_and,
                                      ALU.bitwise_or, ALU.bitwise_xor)
            dve.wait_ge(s_edges, 96)
            V.tensor_scalar(e0[:], src_rows[:], 3, 7, AND, LSL)
            after(V.tensor_scalar(e1[:], src_rows[:], 2, P - 1, LSR, AND))
            V.tensor_scalar(e2[:], src_rows[:], 9, None, LSR)
            after(V.tensor_tensor(pos[:], e0[:], e1[:], OR))
            after(V.tensor_scalar(e0[:], pos[:], 3.0, None, ALU.mult))
            after(V.tensor_scalar(third[:], e0[:], 9, None, LSR))
            after(V.scalar_tensor_tensor(bucket[:], e2[:], 3.0, third[:], ALU.mult, ALU.add))
            V.tensor_scalar(e0[:], bucket[:], 5, None, LSR)
            after(V.tensor_scalar(e1[:], bucket[:], LO - 1, None, AND))
            V.tensor_copy(t16_rows[:], bucket[:]).then_inc(s_rows, 1)
            V.tensor_copy(hi_rows[:], e0[:]).then_inc(s_rows, 1)
            V.tensor_copy(turn[:, 0], bucket[:]).then_inc(s_rows, 1)
            V.tensor_copy(turn[:, 1], e0[:]).then_inc(s_rows, 1)
            V.tensor_copy(turn[:, 2], e1[:]).then_inc(s_rows, 1)
            dve.wait_ge(s_rows, 5)
            V.tensor_scalar(e2[:], dst_rows[:], 5, 16, LSR, LSL)
            after(V.scalar_tensor_tensor(e0[:], third[:], -float(P), pos[:], ALU.mult, ALU.add))
            V.tensor_scalar(word1[:], e2[:], FULL, None, OR)
            V.tensor_scalar(e1[:], dst_rows[:], 31, 24, AND, LSL)
            after(V.tensor_scalar(e0[:], e0[:], 16, FULL, LSL, OR))
            V.tensor_tensor(word2[:], e0[:], e1[:], OR).then_inc(s_rows, 1)
            V.tensor_copy(turn[:, 3], src_rows[:]).then_inc(s_rows, 1)
            V.tensor_copy(turn[:, 4], dst_rows[:]).then_inc(s_rows, 1)
            dve.wait_ge(s_cols, 8)
            V.tensor_copy(hi_col[:], bank[1][:]).then_inc(s_cvt, 1)
            V.tensor_copy(lo_col[:], bank[2][:]).then_inc(s_cvt, 1)
            V.tensor_copy(w2_col[:], bank[6][:]).then_inc(s_cvt, 1)
            V.tensor_copy(src_idx[:], bank[4][:]).then_inc(s_cvt, 1)
            V.tensor_copy(src_col[:], bank[4][:]).then_inc(s_cvt, 1)
            V.tensor_copy(dst_idx[:], bank[5][:]).then_inc(s_cvt, 1)
            dve.wait_ge(s_cvt, 9)
            dve.wait_ge(s_const, 10)

            def hots(k, q, n):
                cols = bass.ds(k * BC, BC)
                V.tensor_tensor(oh_lo[:, cols], lo_col[:, cols].unsqueeze(2).broadcast_to([P, BC, LO]),
                                iota_lo[:].unsqueeze(1).broadcast_to([P, BC, LO]), ALU.is_equal).then_inc(s_ohk, 1)
                V.tensor_tensor(oh_hi[:, cols], hi_col[:, cols].unsqueeze(2).broadcast_to([P, BC, HI]),
                                iota_lo[:, 0:HI].unsqueeze(1).broadcast_to([P, BC, HI]), ALU.is_equal).then_inc(s_ohk, 1)

            batches(dve, hots)
            V.memset(before[:, 0, :], 0.0).then_inc(s_zero, 1)
            V.tensor_copy(earlier16[:], earlier[:])
            V.tensor_scalar(baw[:], b_bc[:], aw[:], None, ALU.mult)
            after(V.tensor_copy(b_parts[:, 0], b_bc[0:3]))
            after(V.tensor_tensor(b_res[:], b_bc[0:3], b_parts[:, 0], ALU.subtract))
            after(V.tensor_copy(b_parts[:, 1], b_res[:]))
            after(V.tensor_tensor(b_acc[:], b_res[:], b_parts[:, 1], ALU.subtract))
            after(V.tensor_copy(b_parts[:, 2], b_acc[:]))
            after(V.tensor_scalar(b_acc[:], b_parts[:, 0], ident[0:3, 0:1], None, ALU.mult))
            after(V.scalar_tensor_tensor(b_res[:], b_parts[:, 1], ident[0:3, 1:2], b_acc[:], ALU.mult, ALU.add))
            after(V.scalar_tensor_tensor(b3[:], b_parts[:, 2], ident[0:3, 2:3], b_res[:], ALU.mult, ALU.add))
            dve.wait_ge(s_histc, B)
            for l in range(LO):
                V.tensor_tensor_scan(before[:, 1:CA + 1, l], ones_scan[:], hist[:, :, l], 0.0, ALU.mult, ALU.add
                                     ).then_inc(s_before, 1)
            dve.wait_ge(s_before, LO)
            V.tensor_reduce(most_hi[:], before[:, CA, :], AX, ALU.max).then_inc(s_mx, 1)

            def rank(k, q, n):
                cols = bass.ds(k * BC, BC)
                V.tensor_copy(t_now[:, q], t_col[:, cols]).then_inc(s_now, 1)
                at_least(dve, s_oh2, k * BC - BC)
                V.tensor_copy(w1_now[:, q], w1_col[:, cols]).then_inc(s_now, 1)
                V.tensor_copy(w2_now[:, q], w2_col[:, cols]).then_inc(s_now, 1)
                dve.wait_ge(s_now, 3 * k + 3)
                dve.wait_ge(s_trow[q], 16 * n + 16)
                for i in range(BC):
                    at_least(dve, s_within, k * BC + (i - 3))
                    V.scalar_tensor_tensor(junk16[:, i % 4], t_row[:, q, i * P:(i + 1) * P], t_now[:, q, i:i + 1], earlier16[:],
                                           ALU.is_equal, ALU.mult, accum_out=within[:, q, i:i + 1]).then_inc(s_within, 1)
                dve.wait_ge(s_q, k + 1)
                V.tensor_tensor(own[:], SORT[q][:, 0:BC * LO].rearrange("p (c l) -> p c l", l=LO),
                                oh_lo[:, cols], ALU.mult).then_inc(s_own, 1)
                dve.wait_ge(s_own, k + 1)
                V.tensor_reduce(base[:], own[:], AX, ALU.add).then_inc(s_base, 1)
                dve.wait_ge(s_base, k + 1)
                dve.wait_ge(s_within, k * BC + BC)
                V.tensor_tensor(slot[:, q], base[:], within[:, q], ALU.add).then_inc(s_slot, 1)
                dve.wait_ge(s_slot, k + 1)
                for i in range(BC):
                    at_least(dve, s_place, k * BC + (i - 3))
                    V.tensor_scalar(oh_t[:, i % 4], iota_nb[:], t_now[:, q, i:i + 1], None, ALU.is_equal).then_inc(s_oh, 1)
                    V.tensor_scalar(oh_s1[:, i % 4], iota_nb[:, 0:P], slot[:, q, i:i + 1], w1_now[:, q, i:i + 1],
                                    ALU.is_equal, ALU.mult).then_inc(s_oh, 1)

            rank(0, 0, 0)
            dve.wait_ge(s_mxT, 1)
            after(V.tensor_reduce(most_all[:], bank[7][0:1, 0:HI], AX, ALU.max))
            V.tensor_scalar(over[:], most_all[:], float(most), None, ALU.is_gt).then_inc(s_over, 1)
            for k in (1, 2):
                rank(k, k % 2, k // 2)
            with dve.Fori(1, (B - 1) // 2) as i:
                rank(i * 2 + 1, 1, i)
                rank(i * 2 + 2, 0, i + 1)

            dve.wait_ge(s_place, CA)
            for half in range(2):
                V.tensor_copy(tab1[:, half * NH:(half + 1) * NH], bank[half][:, 0:NH]).then_inc(s_dec, 1)
                V.tensor_copy(tab2[:, half * NH:(half + 1) * NH], bank[2 + half][:, 0:NH]).then_inc(s_dec, 1)
            dve.wait_ge(s_dec, 4)
            i1, i2 = tab1.bitcast(i32), tab2.bitcast(i32)
            V.tensor_scalar(emp, i1, FULL, FULL, XOR, AND)
            V.tensor_scalar(low5, i2, 31 << 24, 24, AND, LSR)
            after(V.tensor_scalar(tabi[:], i1, 4095 << 16, 11, AND, LSR))
            after(V.tensor_tensor(low5, low5, emp, OR))
            V.memset(node_idx[:, NB:], 0)
            after(V.tensor_tensor(node_idx[:, 0:NB], tabi[:], low5, OR))
            after(V.tensor_scalar(emp, emp, 22, None, LSR))
            after(V.tensor_scalar(tabq[:], i2, 255 << 16, 16, AND, LSR))
            after(V.tensor_tensor(tabi[:], tabq[:], emp, OR))
            after(V.tensor_copy(q_win[:], tabi[:]))

            flag = dve.value_load(over[0:1, 0:1], min_val=0, max_val=1)
            with dve.If(flag):
                with dve.Fori(0, C) as c:
                    mine = src_col[:, bass.ds(c, 1)]
                    V.tensor_copy(now_dst[:], dst_idx[:, bass.ds(c, 1)]).then_inc(z_now, 1)
                    V.tensor_copy(now_src[:], src_idx[:, bass.ds(c, 1)]).then_inc(z_now, 1)
                    dve.wait_ge(z_pT, c + 1)
                    V.tensor_copy(xgT[:], pT).then_inc(z_xgT, 1)
                    V.tensor_scalar(diag[:], ident[:], mine, None, ALU.mult).then_inc(z_xgT, 1)
                    dve.wait_ge(z_msg_ps, c + 1)
                    V.scalar_tensor_tensor(msg[:], pM, aw[:], baw[:], ALU.mult, ALU.add).then_inc(z_msg, 1)
                    V.tensor_scalar(eq[:], pR, mine, None, ALU.is_equal).then_inc(z_eq, 1)
                    dve.wait_ge(z_eq, c + 1)
                    V.scalar_tensor_tensor(junk[:], eq[:], 1.0, earlier[:], ALU.mult, ALU.mult,
                                           accum_out=cnt[:]).then_inc(z_cnt, 1)
                    dve.wait_ge(z_cnt, 3 * c + 1)
                    V.tensor_scalar(skip[:], cnt[:], 1.0, float(1 << 20), ALU.min, ALU.mult).then_inc(z_cnt, 1)
                    dve.wait_ge(z_cnt, 3 * c + 2)
                    V.tensor_tensor(widx[:], skip[:], mine, ALU.add).then_inc(z_cnt, 1)
                    dve.wait_ge(z_comb, c + 1)
                    dve.wait_ge(z_hg, 16 * c + 16)
                    dve.wait_ge(z_cnt, 3 * c + 3)
                    V.tensor_tensor(msg[:], pC, hg[:], ALU.add).then_inc(z_hnew, 1)

                def layernorm(p, g):
                    dve.wait_ge(z_h, 16 * g + 16)
                    hh, qq = h[0:p, 0], xt[0:p, 0]
                    V.tensor_reduce(st[0:p, 0, :], hh, AX, ALU.add).then_inc(z_var, 1)
                    dve.wait_ge(z_var, 5 * g + 1)
                    V.tensor_scalar(st[0:p, 1, :], st[0:p, 0, :], 1.0 / D, None, ALU.mult).then_inc(z_var, 1)
                    dve.wait_ge(z_var, 5 * g + 2)
                    V.tensor_tensor(hh, hh, st[0:p, 1, :].unsqueeze(2).broadcast_to([p, 4, D]), ALU.subtract
                                    ).then_inc(z_var, 1)
                    dve.wait_ge(z_var, 5 * g + 3)
                    V.tensor_tensor(qq, hh, hh, ALU.mult).then_inc(z_sq, 1)
                    dve.wait_ge(z_sq, g + 1)
                    V.tensor_reduce(st[0:p, 2, :], qq, AX, ALU.add).then_inc(z_var, 1)
                    dve.wait_ge(z_var, 5 * g + 4)
                    V.tensor_scalar(st[0:p, 0, :], st[0:p, 2, :], 1.0 / D, EPS, ALU.mult, ALU.add).then_inc(z_var, 1)
                    dve.wait_ge(z_std, 2 * g + 1)
                    V.reciprocal(st[0:p, 2, :], st[0:p, 3, :]).then_inc(z_std, 1)
                    dve.wait_ge(z_std, 2 * g + 2)
                    V.tensor_tensor(hh, hh, st[0:p, 2, :].unsqueeze(2).broadcast_to([p, 4, D]), ALU.mult
                                    ).then_inc(z_norm, 1)

                with dve.Fori(0, G) as g:
                    layernorm(P, g)
                layernorm(PL, G)
            with dve.Else():
                def fetch(g, u, n):
                    at_least(dve, s_agg, g - R + 1)
                    V.tensor_copy(now_idx[:, u], node_idx[:, bass.ds(g * 3, 3)]).then_inc(s_idx, 1)
                    V.tensor_copy(q_now[:, u], q_win[:, bass.ds(g * 3, 3)]).then_inc(s_qn, 1)

                def select(g, u, n):
                    dve.wait_ge(s_qn, g + 1)
                    for k in range(3):
                        V.tensor_scalar(sel[:, u, k], iota_win[:], q_now[:, u, k:k + 1], None, ALU.is_equal
                                        ).then_inc(s_sel, 1)
                        V.tensor_scalar(selh[:, u, k], iota_winh[:], q_now[:, u, k:k + 1], None, ALU.is_equal
                                        ).then_inc(s_sel, 1)

                def add_x(g, u, n):
                    dve.wait_ge(s_out, g + 1)
                    dve.wait_ge(s_x[u], 16 * n + 16)
                    at_least(dve, s_st[u], 16 * n)
                    for j in range(4):
                        V.scalar_tensor_tensor(h[:, u, j], OUT[u % 2][:, j * P:(j + 1) * P], aw[:], xt[:, u, j],
                                               ALU.mult, ALU.add, accum_out=hsum[:, u, j:j + 1]).then_inc(s_h, 1)
                    dve.wait_ge(s_h, 4 * g + 4)
                    V.tensor_scalar(nmean[:, u], hsum[:, u], -1.0 / D, None, ALU.mult).then_inc(s_mean, 1)

                def normalise(g, u, n):
                    dve.wait_ge(s_std, g + 1)
                    V.reciprocal(rstd[:, u], std[:, u]).then_inc(s_rstd, 1)
                    dve.wait_ge(s_rstd, g + 1)
                    for j in range(4):
                        V.tensor_scalar(h[:, u, j], h[:, u, j], nmean[:, u, j:j + 1], rstd[:, u, j:j + 1],
                                        ALU.add, ALU.mult).then_inc(s_y, 1)

                rounds(dve, [(fetch, 0), (select, 1), (add_x, 3), (normalise, 4)])

        @block.scalar
        def _(act):
            act.wait_ge(s_cols, 8)
            nc.scalar.copy(wT[:], bank[7][:, 0:P]).then_inc(s_cvt, 1)
            nc.scalar.copy(t_col[:], bank[0][:]).then_inc(s_cvt, 1)
            nc.scalar.copy(w1_col[:], bank[3][:]).then_inc(s_cvt, 1)

            def keep(k, q, n):
                act.wait_ge(s_hist, k + 1)
                nc.scalar.copy(hist[:, bass.ds(k * BC, BC), :].rearrange("h c l -> h (c l)"), SORT[q][0:HI, :]
                               ).then_inc(s_histc, 1)

            batches(act, keep)

            act.wait_ge(s_over, 1)
            flag = act.value_load(over[0:1, 0:1], min_val=0, max_val=1)
            with act.If(flag):
                def root(p, g):
                    act.wait_ge(z_var, 5 * g + 5)
                    nc.scalar.activation(st[0:p, 3, :], st[0:p, 0, :], ACT.Sqrt).then_inc(z_std, 1)

                with act.Fori(0, G) as g:
                    root(P, g)
                root(PL, G)
            with act.Else():
                def keep_sums(g, u, n):
                    act.wait_ge(s_agg, g + 1)
                    at_least(act, s_out, g - 1)
                    nc.scalar.copy(aggT[:, u % 2], AGG[u % 2][:]).then_inc(s_aggc, 1)
                    nc.scalar.copy(deg[:, u % 2], DEG[u % 2][0:3, :]).then_inc(s_aggc, 1)

                def variance(g, u, n):
                    act.wait_ge(s_mean, g + 1)
                    at_least(act, s_var, 4 * g)
                    for j in range(4):
                        nc.scalar.activation(sq[:, j], h[:, u, j], ACT.Square, bias=nmean[:, u, j:j + 1],
                                             accum_out=vsum[:, u, j:j + 1]).then_inc(s_var, 1)
                    act.wait_ge(s_var, 4 * g + 4)
                    nc.scalar.activation(std[:, u], vsum[:, u], ACT.Sqrt, bias=eps[:], scale=1.0 / D).then_inc(s_std, 1)

                rounds(act, [(keep_sums, 2), (variance, 3)])


_INS = ['x', 'src', 'dst', 'L0_gnn_W', 'L0_gnn_b', 'L0_gnn_agg_weight']


def kernel(**inputs):
    import numpy as _np
    import concourse.bacc as _bacc
    from concourse import mybir as _mybir
    from concourse.bass_utils import run_bass_kernel_spmd as _run

    nc = _bacc.Bacc("TRN2", target_bir_lowering=False, num_devices=1)
    arrays, args = {}, []
    for name in _INS:
        a = _np.ascontiguousarray(inputs[name])
        arrays[f"in_{name}"] = a
        args.append(nc.dram_tensor(f"in_{name}", a.shape, _mybir.dt.from_np(a.dtype), kind="ExternalInput").ap())
    slots = 4 * 128 * 128
    args.append(nc.dram_tensor("t_scratch", (slots,), _mybir.dt.float16, kind="Internal").ap())
    args.append(nc.dram_tensor("hi_scratch", (slots,), _mybir.dt.bfloat16, kind="Internal").ap())
    args.append(nc.dram_tensor("out_0", inputs['x'].shape, _mybir.dt.float32, kind="ExternalOutput").ap())
    gnn_resnorm_kernel(nc, *args)
    r = _run(nc, [arrays], core_ids=[0])
    return r.results[0]["out_0"]
```

```python
import concourse.bass as bass
from concourse import mybir
from contextlib import ExitStack



def gnn_resnorm_kernel(nc, x, src, dst, W, b, agg_weight, hi_scratch, out, most=128):
    f32, i32 = mybir.dt.float32, mybir.dt.int32
    bf16, f16 = mybir.dt.bfloat16, mybir.dt.float16
    ALU, ACT, AX = mybir.AluOpType, mybir.ActivationFunctionType, mybir.AxisListType.X
    P = 128
    N, D = x.shape
    E = src.shape[0]
    GN = 4 * P
    G = N // GN
    PL = (N - G * GN) // 4
    GA = G + 1
    NB = 3 * GA
    NH = NB // 2
    BW = -(-GN // 3)
    SW = BW + BW % 2
    LO = 16
    LO_BITS = 4
    HI = 40
    C = -(-E // P)
    BC = 16
    B = -(-C // BC)
    CA = B * BC
    KB = 4
    PAD = 1 << 17
    FULL = 1 << 30
    RING = 8
    R = 4
    EPS = 1e-5
    assert HI * LO >= NB and 1 << LO_BITS == LO and CA <= KB * P and (B - 1) % 2 == 0 and GA % R == 0 and 3 * GN // 512 == 3

    ctx = ExitStack()
    with ctx:
        def sb(name, shape, dt=f32):
            return ctx.enter_context(nc.sbuf_tensor(name, shape, dt))

        def sem(name):
            return ctx.enter_context(nc.semaphore(name))

        def at_least(eng, s, count):
            if not isinstance(count, int) or count > 0:
                eng.wait_ge(s, count)

        ones = sb("ones", [P, P])
        ident = sb("ident", [P, P])
        earlier = sb("earlier", [P, P])
        later = sb("later", [P, P])
        ident_bf = sb("ident_bf", [P, P], bf16)
        not_earlier = sb("not_earlier", [P, 4, P], bf16)
        iota_nb = sb("iota_nb", [P, NB], f16)
        iota_win = sb("iota_win", [P, SW])
        iota_hi = sb("iota_hi", [P, HI, BC], bf16)
        part = sb("part", [P, 1])
        ones_scan = sb("ones_scan", [HI, CA], bf16)
        ones3 = sb("ones3", [P, 3], bf16)
        eps = sb("eps", [P, 1])
        w_sb = sb("w_sb", [P, P])
        wT = sb("wT", [P, P])
        b_bc = sb("b_bc", [P, D])
        aw = sb("aw", [P, 1])
        b_res = sb("b_res", [3, D])
        b_parts = sb("b_parts", [3, 3, D], bf16)
        b_acc = sb("b_acc", [3, D])
        b3 = sb("b3", [3, D], bf16)
        src_rows = sb("src_rows", [P, KB, P], i32)
        dst_rows = sb("dst_rows", [P, KB, P], i32)
        e0 = sb("e0", [P, KB, P], i32)
        e1 = sb("e1", [P, KB, P], i32)
        e2 = sb("e2", [P, KB, P], i32)
        pos = sb("pos", [P, KB, P], i32)
        third = sb("third", [P, KB, P], i32)
        bucket = sb("bucket", [P, KB, P], i32)
        word1 = sb("word1", [P, KB, P], i32)
        word2 = sb("word2", [P, KB, P], i32)
        hi_rows = sb("hi_rows", [P, KB, P], bf16)
        turn = sb("turn", [P, 5, KB, P])
        t_col = sb("t_col", [P, KB * P])
        hi_col = sb("hi_col", [P, KB * P], bf16)
        lo_col = sb("lo_col", [P, KB * P], bf16)
        w1_col = sb("w1_col", [P, KB * P])
        ratio_col = sb("ratio_col", [P, KB * P])
        w2_col = sb("w2_col", [P, KB * P])
        src_col = sb("src_col", [P, KB * P])
        dst_col = sb("dst_col", [P, KB * P])
        src_idx = sb("src_idx", [P, KB * P], i32)
        dst_idx = sb("dst_idx", [P, KB * P], i32)
        oh_lo = sb("oh_lo", [P, 2, LO, BC], bf16)
        oh_hi = sb("oh_hi", [P, 2, HI, BC], bf16)
        hist = sb("hist", [HI, CA, LO], bf16)
        before = sb("before", [HI, CA + 1, LO], bf16)
        most_hi = sb("most_hi", [HI, 1])
        most_all = sb("most_all", [1, 1])
        over = sb("over", [1, 1], i32)
        hi_row = sb("hi_row", [HI, 2, BC * P], bf16)
        oh_hiT = sb("oh_hiT", [HI, 2, BC * P], bf16)
        before_now = sb("before_now", [HI, 2, BC * LO], bf16)
        t_now = sb("t_now", [P, 2, BC])
        w1_now = sb("w1_now", [P, 2, BC])
        ratio_now = sb("ratio_now", [P, 2, BC])
        same_hi = sb("same_hi", [P, 2, 4, P], bf16)
        own = sb("own", [P, BC, LO], bf16)
        slot = sb("slot", [P, 2, BC])
        oh_t = sb("oh_t", [P, RING, NB], bf16)
        oh_s1 = sb("oh_s1", [P, RING, P], bf16)
        oh_s2 = sb("oh_s2", [P, RING, P], bf16)
        turned = turn[:].rearrange("p a k r -> p (a k r)")
        tab1, tab2 = turned[:, 0:NB], turned[:, NB:2 * NB]
        emp, low5 = (turned[:, i * NB:(i + 1) * NB].bitcast(i32) for i in (2, 3))
        tabi = sb("tabi", [P, NB], i32)
        tabq = sb("tabq", [P, NB], i32)
        table = sb("table", [P, GA, 2, 3], i32)
        now = sb("now", [P, R, 2, 3], i32)
        xg = sb("xg", [P, R, 3, D])
        xt = sb("xt", [P, R, 4, D])
        h = sb("h", [P, R, 4, D])
        y = sb("y", [P, R, 4, D])
        sel = sb("sel", [P, R, 3, SW])
        selh = sel[:].rearrange("p r k n -> p (r k n)").bitcast(bf16).rearrange(
            "p (r k n two) -> p r k n two", r=R, k=3, two=2)[:, :, :, :, 1]
        aggT = sb("aggT", [P, 2, GN])
        deg = sb("deg", [3, 2, GN], bf16)
        stats = sb("stats", [P, R, 4, 6])
        mv = sb("mv", [P, R, 4, 2])
        std = sb("std", [P, R, 4])
        rstd = sb("rstd", [P, R, 4])
        shift = sb("shift", [P, R, 4])
        baw = sb("baw", [P, D])
        xg1 = sb("xg1", [P, D])
        hg = sb("hg", [P, D])
        xgT = sb("xgT", [P, P])
        diag = sb("diag", [P, P])
        eq = sb("eq", [P, P])
        msg = sb("msg", [P, D])
        junk = sb("junk", [P, P])
        cnt = sb("cnt", [P, 1])
        skip = sb("skip", [P, 1])
        widx = sb("widx", [P, 1], i32)
        now_src = sb("now_src", [P, 1], i32)
        now_dst = sb("now_dst", [P, 1], i32)
        st = sb("st", [P, 4, 4])

        bank = [ctx.enter_context(nc.psum_tensor(f"bank{i}", [P, 512], f32)) for i in range(8)]
        SORT = bank[4:6]
        SAME = bank[6:8]
        AGG, OUT, DEG = bank[0:2], bank[2:4], bank[4:6]
        pT, pM, pR, pC = (bank[i][:, 0:P] for i in range(4))

        s_fill = sem("s_fill")
        s_const = sem("s_const")
        s_made = sem("s_made")
        s_edges = sem("s_edges")
        s_w = sem("s_w")
        s_bp = sem("s_bp")
        s_rows = sem("s_rows")
        s_cols = sem("s_cols")
        s_cvt = sem("s_cvt")
        s_scratch = sem("s_scratch")
        s_ohk = sem("s_ohk")
        s_hist = sem("s_hist")
        s_histc = sem("s_histc")
        s_zero = sem("s_zero")
        s_before = sem("s_before")
        s_mx = sem("s_mx")
        s_mxT = sem("s_mxT")
        s_over = sem("s_over")
        s_hrow = [sem(f"s_hrow{i}") for i in range(2)]
        s_hiT = sem("s_hiT")
        s_now = sem("s_now")
        s_lo = sem("s_lo")
        s_bnow = sem("s_bnow")
        s_same = sem("s_same")
        s_samec = sem("s_samec")
        s_q = sem("s_q")
        s_own = sem("s_own")
        s_slot = sem("s_slot")
        s_oh = sem("s_oh")
        s_oh2 = sem("s_oh2")
        s_place = sem("s_place")
        s_clean = sem("s_clean")
        s_dec = sem("s_dec")
        s_idx = sem("s_idx")
        s_g = [sem(f"s_g{i}") for i in range(R)]
        s_x = [sem(f"s_x{i}") for i in range(R)]
        s_st = [sem(f"s_st{i}") for i in range(R)]
        s_sel = sem("s_sel")
        s_agg = sem("s_agg")
        s_aggc = sem("s_aggc")
        s_out = sem("s_out")
        s_h = sem("s_h")
        s_stats = sem("s_stats")
        s_mv = sem("s_mv")
        s_std = sem("s_std")
        s_rstd = sem("s_rstd")
        s_y = sem("s_y")
        z_seed = sem("z_seed")
        z_init = sem("z_init")
        z_xg = sem("z_xg")
        z_hg = sem("z_hg")
        z_pT = sem("z_pT")
        z_xgT = sem("z_xgT")
        z_msg_ps = sem("z_msg_ps")
        z_eq = sem("z_eq")
        z_msg = sem("z_msg")
        z_comb = sem("z_comb")
        z_hnew = sem("z_hnew")
        z_now = sem("z_now")
        z_cnt = sem("z_cnt")
        z_scat = sem("z_scat")
        z_h = sem("z_h")
        z_sq = sem("z_sq")
        z_var = sem("z_var")
        z_std = sem("z_std")
        z_norm = sem("z_norm")
        z_store = sem("z_store")

        def batches(eng, step):
            for k in range(3):
                step(k, k % 2, k // 2)
            with eng.Fori(1, (B - 1) // 2) as i:
                step(i * 2 + 1, 1, i)
                step(i * 2 + 2, 0, i + 1)

        def lagging(eng, first, second):
            def both(k, q, n):
                first(k, q, n, lambda lo, hi: None if isinstance(k, int) and k == 0 else second(k - 1, 1 - q, lo, hi))

            batches(eng, both)
            second(B - 1, (B - 1) % 2, 0, C - (B - 1) * BC)

        def rounds(eng, stages):
            def static(i):
                for stage, lag in stages:
                    if 0 <= i - lag < GA:
                        stage(i - lag, (i - lag) % R, (i - lag) // R)

            for i in range(SPAN * R):
                static(i)
            with eng.Fori(1, (GA // R - 1) // SPAN) as many:
                for u in range(SPAN * R):
                    for stage, lag in stages:
                        stage(many * (SPAN * R) + (u - lag), (u - lag) % R, many * SPAN + (u - lag) // R)
            for i in range(GA - R, GA + max(lag for _, lag in stages)):
                static(i)

        SPAN = 4
        assert (GA // R - 1) % SPAN == 0

        block = ctx.enter_context(nc.Block())

        @block.sync
        def _(sp):
            sp.wait_ge(s_fill, 2)
            full = E // (P * P)
            r = (E - full * P * P) // P
            done = (full * P + r) * P
            for rows, arr in ((src_rows, src), (dst_rows, dst)):
                sp.dma_start(rows[:, 0:full, :], arr[0:full * P * P].rearrange("(k r p) -> r k p", r=P, p=P)
                             ).then_inc(s_edges, 16)
                sp.dma_start(rows[0:r, full, :], arr[full * P * P:done].rearrange("(r p) -> r p", p=P)
                             ).then_inc(s_edges, 16)
                sp.dma_start(rows[r:r + 1, full, 0:E - done], arr[done:E].rearrange("(r p) -> r p", r=1)
                             ).then_inc(s_edges, 16)
            sp.dma_start(w_sb[:], W).then_inc(s_w, 16)
            sp.dma_start(b_bc[:], b.rearrange("(o d) -> o d", o=1).broadcast_to([P, D])).then_inc(s_w, 16)
            sp.dma_start(aw[:], agg_weight.rearrange("(o d) -> o d", o=1).broadcast_to([P, 1])).then_inc(s_w, 16)
            sp.wait_ge(s_rows, 1)
            sp.dma_start(hi_scratch.rearrange("(k r p) -> r k p", r=P, p=P), hi_rows[:]).then_inc(s_scratch, 16)
            sp.wait_ge(s_scratch, 16)

            def load_rows(k, q, n):
                at_least(sp, s_hiT, k - 1)
                sp.dma_start(hi_row[:, q], hi_scratch[bass.ds(k * (BC * P), BC * P)].rearrange(
                    "(o n) -> o n", o=1).broadcast_to([HI, BC * P])).then_inc(s_hrow[q], 16)

            load_rows(0, 0, 0)
            load_rows(1, 1, 0)
            with sp.Fori(1, (B - 1) // 2) as i:
                load_rows(i * 2, 0, i)
                load_rows(i * 2 + 1, 1, i)
            load_rows(B - 1, 0, (B - 1) // 2)

            sp.wait_ge(s_over, 1)
            flag = sp.value_load(over[0:1, 0:1], min_val=0, max_val=1)
            with sp.If(flag):
                sp.dma_start(out.rearrange("(a n) d -> a (n d)", a=16), x.rearrange("(a n) d -> a (n d)", a=16)
                             ).then_inc(z_seed, 16)
                sp.wait_ge(z_scat, 16 * C)
                sp.sem_inc(z_store, 16)

                def pass_group(g, rows, p):
                    sp.wait_ge(z_store, g * 16 + 16)
                    sp.dma_start(h[0:p, 0], rows).then_inc(z_h, 16)
                    sp.wait_ge(z_norm, g + 1)
                    sp.dma_start(rows, h[0:p, 0]).then_inc(z_store, 16)

                with sp.Fori(0, G) as g:
                    pass_group(g, out[bass.ds(g * GN, GN), :].rearrange("(p j) d -> p j d", j=4), P)
                pass_group(G, out[G * GN:N, :].rearrange("(p j) d -> p j d", j=4), PL)
                sp.wait_ge(z_store, G * 16 + 32)
            with sp.Else():
                sp.wait_ge(s_clean, 2)

                def load(g, u, n):
                    at_least(sp, s_h, g - R + 1)
                    if isinstance(g, int) and g == G:
                        sp.dma_start(xt[0:PL, u], x[G * GN:N, :].rearrange("(p j) d -> p j d", j=4)).then_inc(s_x[u], 16)
                    else:
                        sp.dma_start(xt[:, u], x[bass.ds(g * GN, GN), :].rearrange("(p j) d -> p j d", j=4)
                                     ).then_inc(s_x[u], 16)

                def store(g, u, n):
                    sp.wait_ge(s_y, 4 * g + 4)
                    if isinstance(g, int) and g == G:
                        sp.dma_start(out[G * GN:N, :].rearrange("(p j) d -> p j d", j=4), y[0:PL, u]).then_inc(s_st[u], 16)
                    else:
                        sp.dma_start(out[bass.ds(g * GN, GN), :].rearrange("(p j) d -> p j d", j=4), y[:, u]
                                     ).then_inc(s_st[u], 16)

                rounds(sp, [(load, 0), (store, 7)])
                for u in range(R):
                    sp.wait_ge(s_st[u], 16 * (GA // R))

        @block.gpsimd
        def _(pool):
            nc.gpsimd.memset(src_rows[:], PAD).then_inc(s_fill, 1)
            nc.gpsimd.memset(dst_rows[:], PAD).then_inc(s_fill, 1)
            nc.gpsimd.memset(ones[:], 1.0).then_inc(s_made, 1)
            nc.gpsimd.iota(iota_hi[:], [[1, HI], [0, BC]], base=0, channel_multiplier=0,
                           allow_small_or_imprecise_dtypes=True).then_inc(s_const, 1)
            nc.gpsimd.iota(part[:], [[0, 1]], base=0, channel_multiplier=1,
                           allow_small_or_imprecise_dtypes=True).then_inc(s_const, 1)
            pool.wait_ge(s_made, 1)
            nc.gpsimd.affine_select(out=ident[:], in_=ones[:], compare_op=ALU.is_equal, fill=0.0, base=0,
                                    pattern=[[-1, P]], channel_multiplier=1).then_inc(s_const, 1)
            nc.gpsimd.affine_select(out=earlier[:], in_=ones[:], compare_op=ALU.is_gt, fill=0.0, base=0,
                                    pattern=[[-1, P]], channel_multiplier=1).then_inc(s_const, 1)
            nc.gpsimd.affine_select(out=later[:], in_=ones[:], compare_op=ALU.is_gt, fill=0.0, base=0,
                                    pattern=[[1, P]], channel_multiplier=-1).then_inc(s_const, 1)
            nc.gpsimd.iota(iota_nb[:], [[1, NB]], base=0, channel_multiplier=0,
                           allow_small_or_imprecise_dtypes=True).then_inc(s_const, 1)
            nc.gpsimd.iota(iota_win[:], [[1, SW]], base=0, channel_multiplier=0,
                           allow_small_or_imprecise_dtypes=True).then_inc(s_const, 1)
            nc.gpsimd.memset(eps[:], EPS).then_inc(s_const, 1)
            nc.gpsimd.memset(ones3[:], 1.0).then_inc(s_const, 1)
            nc.gpsimd.memset(ones_scan[:], 1.0).then_inc(s_const, 1)
            nc.gpsimd.memset(xg1[:], 0.0).then_inc(z_init, 1)
            nc.gpsimd.memset(hg[:], 0.0).then_inc(z_init, 1)
            pool.wait_ge(s_const, 10)

            pool.wait_ge(s_cvt, 8)
            nc.gpsimd.tensor_copy(src_idx[:], src_col[:]).then_inc(z_init, 1)
            nc.gpsimd.tensor_copy(dst_idx[:], dst_col[:]).then_inc(z_init, 1)
            nc.gpsimd.memset(xt[:], 0.0).then_inc(s_clean, 1)
            nc.gpsimd.memset(xg[:], 0.0).then_inc(s_clean, 1)

            def one_hots(k, q, n):
                pool.wait_ge(s_hrow[q], 16 * n + 16)
                at_least(pool, s_q, k - 1)
                pool.nop(nofuse=True)
                nc.gpsimd.tensor_scalar(oh_hiT[:, q], hi_row[:, q], part[0:HI], None, ALU.is_equal).then_inc(s_hiT, 1)

            batches(pool, one_hots)

            pool.wait_ge(s_over, 1)
            flag = pool.value_load(over[0:1, 0:1], min_val=0, max_val=1)
            last_node = pool.to_reg(N - 1)
            with pool.If(flag):
                pool.wait_ge(z_seed, 16)
                pool.wait_ge(z_init, 4)
                with pool.Fori(0, C) as c:
                    pool.wait_ge(z_now, 2 * c + 2)
                    pool.nop(nofuse=True)
                    nc.gpsimd.indirect_dma_start(
                        out=xg1[:], out_offset=None, in_=x, in_offset=bass.IndirectOffsetOnAxis(ap=now_dst[:], axis=0),
                        bounds_check=last_node, oob_is_err=False).then_inc(z_xg, 16)
                    nc.gpsimd.indirect_dma_start(
                        out=hg[:], out_offset=None, in_=out, in_offset=bass.IndirectOffsetOnAxis(ap=now_src[:], axis=0),
                        bounds_check=last_node, oob_is_err=False).then_inc(z_hg, 16)
                    pool.wait_ge(z_hnew, c + 1)
                    pool.nop(nofuse=True)
                    nc.gpsimd.indirect_dma_start(
                        out=out, out_offset=bass.IndirectOffsetOnAxis(ap=widx[:], axis=0), in_=msg[:], in_offset=None,
                        bounds_check=last_node, oob_is_err=False).then_inc(z_scat, 16)
                    pool.wait_ge(z_scat, c * 16 + 16)
                    pool.nop(nofuse=True)
            with pool.Else():
                pool.wait_ge(s_clean, 2)

                def gather(g, u, n):
                    pool.wait_ge(s_idx, g + 1)
                    pool.nop(nofuse=True)
                    for k in range(3):
                        nc.gpsimd.indirect_dma_start(
                            out=xg[:, u, k], out_offset=None, in_=x,
                            in_offset=bass.IndirectOffsetOnAxis(ap=now[:, u, 0, k:k + 1], axis=0),
                            bounds_check=last_node, oob_is_err=False).then_inc(s_g[u], 16)

                rounds(pool, [(gather, 0)])

        @block.tensor
        def _(pe):
            pe.wait_ge(s_const, 4)
            pe.wait_ge(s_w, 48)
            nc.tensor.transpose(bank[7][:, 0:P], w_sb[:], ident[:]).then_inc(s_cols, 1)
            pe.wait_ge(s_rows, 7)
            for j, rows in enumerate((turn[:, 0], turn[:, 1], turn[:, 2], word1[:].bitcast(f32), turn[:, 3],
                                      turn[:, 4], word2[:].bitcast(f32))):
                for k in range(KB):
                    last = nc.tensor.transpose(bank[j][:, k * P:(k + 1) * P], rows[:, k, :], ident[:])
                last.then_inc(s_cols, 1)
            pe.wait_ge(s_cvt, 8)

            def histogram(k, q, n):
                pe.wait_ge(s_ohk, k + 1)
                pe.wait_ge(s_lo, k + 1)
                at_least(pe, s_histc, k - 1)
                for i in range(BC):
                    last = nc.tensor.matmul(SORT[q][0:HI, i * LO:(i + 1) * LO], oh_hi[:, q, :, i], oh_lo[:, q, :, i],
                                            start=True, stop=True)
                last.then_inc(s_hist, 1)

            batches(pe, histogram)
            pe.wait_ge(s_mx, 1)
            nc.tensor.transpose(bank[0][0:1, 0:HI], most_hi[:], ident[0:HI, 0:HI]).then_inc(s_mxT, 1)
            pe.wait_ge(s_histc, B)

            def count(k, q, n, place_some):
                hot = lambda i: oh_hiT[:, q, i * P:(i + 1) * P]

                def same(c):
                    at_least(pe, s_samec, k * 4 + (c - 1))
                    nc.tensor.matmul(SAME[c % 2][:], ident_bf[:], not_earlier[:].rearrange("p c e -> p (c e)"),
                                     start=True, stop=False, skip_group_check=True)
                    for j in range(4):
                        last = nc.tensor.matmul(SAME[c % 2][:, j * P:(j + 1) * P], hot(4 * c + j), hot(4 * c + j),
                                                start=False, stop=True, skip_group_check=True)
                    last.then_inc(s_same, 1)

                def add(c):
                    pe.wait_ge(s_samec, k * 4 + (c + 1))
                    for j in range(4):
                        i = 4 * c + j
                        counts = SORT[q][:, i * LO:(i + 1) * LO]
                        nc.tensor.matmul(counts, hot(i), before_now[:, q, i * LO:(i + 1) * LO], start=True, stop=False,
                                         skip_group_check=True)
                        last = nc.tensor.matmul(counts, same_hi[:, c % 2, j], oh_lo[:, q, :, i], start=False, stop=True,
                                                skip_group_check=True)
                    return last

                pe.wait_ge(s_hiT, k + 1)
                same(0)
                same(1)
                place_some(0, 4)
                pe.wait_ge(s_bnow, k + 1)
                pe.wait_ge(s_lo, k + (B + 1))
                at_least(pe, s_own, k - 1)
                add(0)
                same(2)
                add(1)
                same(3)
                place_some(4, 8)
                add(2)
                add(3).then_inc(s_q, 1)
                place_some(8, BC)

            def place(k, q, lo, hi):
                for i in range(lo, hi):
                    pe.wait_ge(s_oh, k * (2 * BC) + (2 * i + 2))
                    pe.wait_ge(s_oh2, k * BC + (i + 1))
                    first = isinstance(k, int) and k == 0 and i == 0
                    for w, hot in ((0, oh_s1[:, i % RING]), (1, oh_s2[:, i % RING])):
                        for half in range(2):
                            last = nc.tensor.matmul(bank[2 * w + half][:, 0:NH], hot,
                                                    oh_t[:, i % RING, half * NH:(half + 1) * NH], start=first, stop=False,
                                                    skip_group_check=True)
                    last.then_inc(s_place, 1)

            lagging(pe, count, place)

            pe.wait_ge(s_over, 1)
            flag = pe.value_load(over[0:1, 0:1], min_val=0, max_val=1)
            with pe.If(flag):
                pe.wait_ge(s_dec, 4)
                with pe.Fori(0, C) as c:
                    pe.wait_ge(z_xg, 16 * c + 16)
                    nc.tensor.transpose(pT, xg1[:], ident[:]).then_inc(z_pT, 1)
                    pe.wait_ge(z_xgT, 2 * c + 2)
                    nc.tensor.matmul(pR, ones[:], diag[:], start=True, stop=True)
                    nc.tensor.matmul(pM, xgT[:], wT[:], start=True, stop=True).then_inc(z_msg_ps, 1)
                    pe.wait_ge(z_msg, c + 1)
                    pe.wait_ge(z_eq, c + 1)
                    nc.tensor.matmul(pC, eq[:], msg[:], start=True, stop=True).then_inc(z_comb, 1)
            with pe.Else():
                pe.wait_ge(s_dec, 4)

                def aggregate(g, u, n):
                    pe.wait_ge(s_g[u], 48 * n + 48)
                    pe.wait_ge(s_sel, 3 * g + 3)
                    at_least(pe, s_aggc, 2 * g - 2)
                    q = u % 2
                    for k in range(3):
                        lo, hi = k * BW, min(k * BW + BW, GN)
                        nc.tensor.matmul(AGG[q][:, lo:hi], xg[:, u, k], sel[:, u, k, 0:hi - lo],
                                         start=(k == 0), stop=(k == 2), skip_group_check=True)
                    for k in range(3):
                        lo, hi = k * BW, min(k * BW + BW, GN)
                        last = nc.tensor.matmul(DEG[q][0:3, lo:hi], ones3[:], selh[:, u, k, 0:hi - lo],
                                                start=(k == 0), stop=(k == 2), skip_group_check=True)
                    last.then_inc(s_agg, 1)

                def project(g, u, n):
                    pe.wait_ge(s_aggc, 2 * g + 2)
                    at_least(pe, s_h, g - 1)
                    q = u % 2
                    for j in range(4):
                        nodes = slice(j * P, (j + 1) * P)
                        nc.tensor.matmul(OUT[q][:, nodes], aggT[:, q, nodes], wT[:], start=(j == 0), stop=False,
                                         skip_group_check=True)
                        last = nc.tensor.matmul(OUT[q][:, nodes], deg[:, q, nodes], b3[:], start=False, stop=True,
                                                skip_group_check=True)
                    last.then_inc(s_out, 1)

                rounds(pe, [(aggregate, 0), (project, 1)])

        @block.vector
        def _(dve):
            step_no = [0]

            def after(ins):
                step_no[0] += 1
                ins.then_inc(s_bp, 1)
                dve.wait_ge(s_bp, step_no[0])

            V = nc.vector
            LSR, LSL, AND, OR, XOR = (ALU.logical_shift_right, ALU.logical_shift_left, ALU.bitwise_and,
                                      ALU.bitwise_or, ALU.bitwise_xor)
            dve.wait_ge(s_edges, 96)
            V.tensor_scalar(e0[:], src_rows[:], 3, 7, AND, LSL)
            after(V.tensor_scalar(e1[:], src_rows[:], 2, P - 1, LSR, AND))
            V.tensor_scalar(e2[:], src_rows[:], 9, None, LSR)
            after(V.tensor_tensor(pos[:], e0[:], e1[:], OR))
            after(V.tensor_scalar(e0[:], pos[:], 3.0, None, ALU.mult))
            after(V.tensor_scalar(third[:], e0[:], 9, None, LSR))
            after(V.scalar_tensor_tensor(bucket[:], e2[:], 3.0, third[:], ALU.mult, ALU.add))
            V.tensor_scalar(e0[:], bucket[:], LO_BITS, None, LSR)
            after(V.tensor_scalar(e1[:], bucket[:], LO - 1, None, AND))
            V.tensor_copy(hi_rows[:], e0[:]).then_inc(s_rows, 1)
            V.tensor_copy(turn[:, 0], bucket[:]).then_inc(s_rows, 1)
            V.tensor_copy(turn[:, 1], e0[:]).then_inc(s_rows, 1)
            V.tensor_copy(turn[:, 2], e1[:]).then_inc(s_rows, 1)
            dve.wait_ge(s_rows, 4)
            V.tensor_scalar(e2[:], dst_rows[:], 5, 16, LSR, LSL)
            after(V.scalar_tensor_tensor(e0[:], third[:], -float(BW), pos[:], ALU.mult, ALU.add))
            V.tensor_scalar(word1[:], e2[:], FULL, None, OR)
            V.tensor_scalar(e1[:], dst_rows[:], 31, 24, AND, LSL)
            after(V.tensor_scalar(e0[:], e0[:], 16, FULL, LSL, OR))
            V.tensor_tensor(word2[:], e0[:], e1[:], OR).then_inc(s_rows, 1)
            V.tensor_copy(turn[:, 3], src_rows[:]).then_inc(s_rows, 1)
            V.tensor_copy(turn[:, 4], dst_rows[:]).then_inc(s_rows, 1)
            dve.wait_ge(s_cols, 8)
            V.tensor_copy(w1_col[:], bank[3][:]).then_inc(s_cvt, 1)
            V.tensor_copy(hi_col[:], bank[1][:]).then_inc(s_cvt, 1)
            V.tensor_copy(lo_col[:], bank[2][:]).then_inc(s_cvt, 1)
            dve.wait_ge(s_cvt, 8)
            dve.wait_ge(s_const, 10)

            def low_hots(k, q):
                V.tensor_tensor(oh_lo[:, q], lo_col[:, bass.ds(k * BC, BC)].unsqueeze(1).broadcast_to([P, LO, BC]),
                                iota_hi[:, 0:LO], ALU.is_equal).then_inc(s_lo, 1)

            def hots(k, q, n):
                at_least(dve, s_hist, k - 1)
                low_hots(k, q)
                V.tensor_tensor(oh_hi[:, q], hi_col[:, bass.ds(k * BC, BC)].unsqueeze(1).broadcast_to([P, HI, BC]),
                                iota_hi[:], ALU.is_equal).then_inc(s_ohk, 1)

            batches(dve, hots)
            V.memset(before[:, 0, :], 0.0).then_inc(s_zero, 1)
            V.tensor_copy(ident_bf[:], ident[:]).then_inc(s_zero, 1)
            V.tensor_scalar(not_earlier[:], later[:].unsqueeze(1).broadcast_to([P, 4, P]), -1.0, None, ALU.add
                            ).then_inc(s_zero, 1)
            dve.wait_ge(s_histc, B)
            for l in range(LO):
                V.tensor_tensor_scan(before[:, 1:CA + 1, l], ones_scan[:], hist[:, :, l], 0.0, ALU.mult, ALU.add
                                     ).then_inc(s_before, 1)
            dve.wait_ge(s_before, LO)
            V.tensor_reduce(most_hi[:], before[:, CA, :], AX, ALU.max).then_inc(s_mx, 1)

            def rank(k, q, n, hots_some):
                cols = bass.ds(k * BC, BC)
                at_least(dve, s_oh, (k - 1) * (2 * BC))
                at_least(dve, s_oh2, k * BC - BC)
                V.tensor_copy(t_now[:, q], t_col[:, cols]).then_inc(s_now, 1)
                V.tensor_copy(w1_now[:, q], w1_col[:, cols]).then_inc(s_now, 1)
                at_least(dve, s_q, k - 1)
                low_hots(k, q)
                if isinstance(k, int) and k == 0:
                    after(V.reciprocal(ratio_col[:], w1_col[:]))
                    after(V.tensor_tensor(ratio_col[:], w2_col[:], ratio_col[:], ALU.mult))
                V.tensor_copy(ratio_now[:, q], ratio_col[:, cols]).then_inc(s_now, 1)
                hots_some(0, BC)
                dve.wait_ge(s_q, k + 1)
                V.tensor_tensor(own[:], SORT[q][:, 0:BC * LO].rearrange("p (c l) -> p c l", l=LO),
                                oh_lo[:, q].rearrange("p l c -> p c l"), ALU.mult).then_inc(s_own, 1)
                dve.wait_ge(s_own, k + 1)
                V.tensor_reduce(slot[:, q], own[:], AX, ALU.add).then_inc(s_slot, 1)

            def spread(k, q, lo, hi):
                dve.wait_ge(s_slot, k + 1)
                for i in range(lo, hi):
                    at_least(dve, s_place, k * BC + (i - RING + 1))
                    V.tensor_scalar(oh_s1[:, i % RING], iota_nb[:, 0:P], slot[:, q, i:i + 1], w1_now[:, q, i:i + 1],
                                    ALU.is_equal, ALU.mult).then_inc(s_oh, 1)
                    V.tensor_scalar(oh_t[:, i % RING], iota_nb[:], t_now[:, q, i:i + 1], None, ALU.is_equal).then_inc(s_oh, 1)

            dve.wait_ge(s_mxT, 1)
            after(V.tensor_reduce(most_all[:], bank[0][0:1, 0:HI], AX, ALU.max))
            V.tensor_scalar(over[:], most_all[:], float(most), None, ALU.is_gt).then_inc(s_over, 1)
            lagging(dve, rank, spread)

            V.tensor_scalar(baw[:], b_bc[:], aw[:], None, ALU.mult)
            after(V.tensor_copy(b_parts[:, 0], b_bc[0:3]))
            after(V.tensor_tensor(b_res[:], b_bc[0:3], b_parts[:, 0], ALU.subtract))
            after(V.tensor_copy(b_parts[:, 1], b_res[:]))
            after(V.tensor_tensor(b_acc[:], b_res[:], b_parts[:, 1], ALU.subtract))
            after(V.tensor_copy(b_parts[:, 2], b_acc[:]))
            after(V.tensor_scalar(b_acc[:], b_parts[:, 0], ident[0:3, 0:1], None, ALU.mult))
            after(V.scalar_tensor_tensor(b_res[:], b_parts[:, 1], ident[0:3, 1:2], b_acc[:], ALU.mult, ALU.add))
            after(V.scalar_tensor_tensor(b3[:], b_parts[:, 2], ident[0:3, 2:3], b_res[:], ALU.mult, ALU.add))

            dve.wait_ge(s_place, C)
            for half in range(2):
                V.tensor_copy(tab1[:, half * NH:(half + 1) * NH], bank[half][:, 0:NH]).then_inc(s_dec, 1)
                V.tensor_copy(tab2[:, half * NH:(half + 1) * NH], bank[2 + half][:, 0:NH]).then_inc(s_dec, 1)
            dve.wait_ge(s_dec, 4)
            i1, i2 = tab1.bitcast(i32), tab2.bitcast(i32)
            V.tensor_scalar(emp, i1, FULL, FULL, XOR, AND)
            V.tensor_scalar(low5, i2, 31 << 24, 24, AND, LSR)
            after(V.tensor_scalar(tabi[:], i1, 4095 << 16, 11, AND, LSR))
            after(V.tensor_tensor(low5, low5, emp, OR))
            by3 = lambda t: t.rearrange("p (g k) -> p g k", k=3)
            after(V.tensor_tensor(table[:, :, 0], by3(tabi[:]), by3(low5), OR))
            after(V.tensor_scalar(emp, emp, 22, None, LSR))
            after(V.tensor_scalar(tabq[:], i2, 255 << 16, 16, AND, LSR))
            after(V.tensor_tensor(table[:, :, 1], by3(tabq[:]), by3(emp), OR))

            flag = dve.value_load(over[0:1, 0:1], min_val=0, max_val=1)
            with dve.If(flag):
                dve.wait_ge(z_init, 4)
                with dve.Fori(0, C) as c:
                    mine = src_col[:, bass.ds(c, 1)]
                    V.tensor_copy(now_dst[:], dst_idx[:, bass.ds(c, 1)]).then_inc(z_now, 1)
                    V.tensor_copy(now_src[:], src_idx[:, bass.ds(c, 1)]).then_inc(z_now, 1)
                    dve.wait_ge(z_pT, c + 1)
                    V.tensor_copy(xgT[:], pT).then_inc(z_xgT, 1)
                    V.tensor_scalar(diag[:], ident[:], mine, None, ALU.mult).then_inc(z_xgT, 1)
                    dve.wait_ge(z_msg_ps, c + 1)
                    V.scalar_tensor_tensor(msg[:], pM, aw[:], baw[:], ALU.mult, ALU.add).then_inc(z_msg, 1)
                    V.tensor_scalar(eq[:], pR, mine, None, ALU.is_equal).then_inc(z_eq, 1)
                    dve.wait_ge(z_eq, c + 1)
                    V.scalar_tensor_tensor(junk[:], eq[:], 1.0, earlier[:], ALU.mult, ALU.mult,
                                           accum_out=cnt[:]).then_inc(z_cnt, 1)
                    dve.wait_ge(z_cnt, 3 * c + 1)
                    V.tensor_scalar(skip[:], cnt[:], 1.0, float(1 << 20), ALU.min, ALU.mult).then_inc(z_cnt, 1)
                    dve.wait_ge(z_cnt, 3 * c + 2)
                    V.tensor_tensor(widx[:], skip[:], mine, ALU.add).then_inc(z_cnt, 1)
                    dve.wait_ge(z_comb, c + 1)
                    dve.wait_ge(z_hg, 16 * c + 16)
                    dve.wait_ge(z_cnt, 3 * c + 3)
                    V.tensor_tensor(msg[:], pC, hg[:], ALU.add).then_inc(z_hnew, 1)

                def layernorm(p, g):
                    dve.wait_ge(z_h, 16 * g + 16)
                    hh, qq = h[0:p, 0], xt[0:p, 0]
                    V.tensor_reduce(st[0:p, 0, :], hh, AX, ALU.add).then_inc(z_var, 1)
                    dve.wait_ge(z_var, 5 * g + 1)
                    V.tensor_scalar(st[0:p, 1, :], st[0:p, 0, :], 1.0 / D, None, ALU.mult).then_inc(z_var, 1)
                    dve.wait_ge(z_var, 5 * g + 2)
                    V.tensor_tensor(hh, hh, st[0:p, 1, :].unsqueeze(2).broadcast_to([p, 4, D]), ALU.subtract
                                    ).then_inc(z_var, 1)
                    dve.wait_ge(z_var, 5 * g + 3)
                    V.tensor_tensor(qq, hh, hh, ALU.mult).then_inc(z_sq, 1)
                    dve.wait_ge(z_sq, g + 1)
                    V.tensor_reduce(st[0:p, 2, :], qq, AX, ALU.add).then_inc(z_var, 1)
                    dve.wait_ge(z_var, 5 * g + 4)
                    V.tensor_scalar(st[0:p, 0, :], st[0:p, 2, :], 1.0 / D, EPS, ALU.mult, ALU.add).then_inc(z_var, 1)
                    dve.wait_ge(z_std, 2 * g + 1)
                    V.reciprocal(st[0:p, 2, :], st[0:p, 3, :]).then_inc(z_std, 1)
                    dve.wait_ge(z_std, 2 * g + 2)
                    V.tensor_tensor(hh, hh, st[0:p, 2, :].unsqueeze(2).broadcast_to([p, 4, D]), ALU.mult
                                    ).then_inc(z_norm, 1)

                with dve.Fori(0, G) as g:
                    layernorm(P, g)
                layernorm(PL, G)
            with dve.Else():
                def fetch(g, u, n):
                    at_least(dve, s_agg, g - R + 1)
                    V.tensor_copy(now[:, u].rearrange("p w k -> p (w k)"),
                                  table[:, bass.ds(g, 1)].rearrange("p g w k -> p (g w k)")).then_inc(s_idx, 1)

                def select(g, u, n):
                    dve.wait_ge(s_idx, g + 1)
                    for k in range(3):
                        V.tensor_scalar(sel[:, u, k], iota_win[:], now[:, u, 1, k:k + 1], None, ALU.is_equal
                                        ).then_inc(s_sel, 1)

                def add_x(g, u, n):
                    dve.wait_ge(s_out, g + 1)
                    dve.wait_ge(s_x[u], 16 * n + 16)
                    at_least(dve, s_y, 4 * g - 4 * R + 4)
                    V.scalar_tensor_tensor(h[:, u].rearrange("p j d -> p (j d)"), OUT[u % 2][:], aw[:],
                                           xt[:, u].rearrange("p j d -> p (j d)"), ALU.mult, ALU.add).then_inc(s_h, 1)

                def moments(g, u, n):
                    dve.wait_ge(s_h, g + 1)
                    for j in range(4):
                        V.bn_stats(stats[:, u, j], h[:, u, j]).then_inc(s_stats, 1)

                def combine(g, u, n):
                    dve.wait_ge(s_stats, 4 * g + 4)
                    dve.nop(nofuse=True)
                    for j in range(4):
                        V.bn_aggr(mv[:, u, j], stats[:, u, j]).then_inc(s_mv, 1)

                def invert(g, u, n):
                    dve.wait_ge(s_std, g + 1)
                    V.reciprocal(rstd[:, u], std[:, u]).then_inc(s_rstd, 1)

                def recentre(g, u, n):
                    dve.wait_ge(s_rstd, 2 * g + 1)
                    V.scalar_tensor_tensor(shift[:, u], mv[:, u, :, 0], -1.0, rstd[:, u], ALU.mult, ALU.mult
                                           ).then_inc(s_rstd, 1)

                rounds(dve, [(fetch, 0), (add_x, 5), (select, 2), (moments, 5), (invert, 6), (combine, 5),
                             (recentre, 6)])

        @block.scalar
        def _(act):
            act.wait_ge(s_cols, 8)
            nc.scalar.copy(wT[:], bank[7][:, 0:P]).then_inc(s_cvt, 1)
            for column, turned_back in ((src_col, bank[4]), (dst_col, bank[5]), (t_col, bank[0]), (w2_col, bank[6])):
                nc.scalar.copy(column[:], turned_back[:]).then_inc(s_cvt, 1)

            def keep(k, q, n):
                act.wait_ge(s_hist, k + 1)
                nc.scalar.copy(hist[:, bass.ds(k * BC, BC), :].rearrange("h c l -> h (c l)"), SORT[q][0:HI, 0:BC * LO]
                               ).then_inc(s_histc, 1)

            batches(act, keep)

            def clip(k, q, n, scale_some):
                at_least(act, s_q, k - 1)
                act.wait_ge(s_before, LO)
                nc.scalar.copy(before_now[:, q], before[:, bass.ds(k * BC, BC)].rearrange("h c l -> h (c l)")
                               ).then_inc(s_bnow, 1)

                def same(c):
                    act.wait_ge(s_same, k * 4 + (c + 1))
                    nc.scalar.activation(same_hi[:, c % 2].rearrange("p j e -> p (j e)"), SAME[c % 2][:], ACT.Relu
                                         ).then_inc(s_samec, 1)

                scale_some(0, 4)
                same(0)
                same(1)
                scale_some(4, 8)
                same(2)
                same(3)
                scale_some(8, BC)

            def second_word(k, q, lo, hi):
                for i in range(lo, hi):
                    act.wait_ge(s_oh, k * (2 * BC) + (2 * i + 1))
                    at_least(act, s_place, k * BC + (i - RING + 1))
                    nc.scalar.activation(oh_s2[:, i % RING], oh_s1[:, i % RING], ACT.Copy, scale=ratio_now[:, q, i:i + 1]
                                         ).then_inc(s_oh2, 1)

            lagging(act, clip, second_word)

            act.wait_ge(s_over, 1)
            flag = act.value_load(over[0:1, 0:1], min_val=0, max_val=1)
            with act.If(flag):
                def root(p, g):
                    act.wait_ge(z_var, 5 * g + 5)
                    nc.scalar.activation(st[0:p, 3, :], st[0:p, 0, :], ACT.Sqrt).then_inc(z_std, 1)

                with act.Fori(0, G) as g:
                    root(P, g)
                root(PL, G)
            with act.Else():
                def keep_sums(g, u, n):
                    act.wait_ge(s_agg, g + 1)
                    at_least(act, s_out, g - 1)
                    nc.scalar.copy(aggT[:, u % 2], AGG[u % 2][:]).then_inc(s_aggc, 1)
                    nc.scalar.copy(deg[:, u % 2], DEG[u % 2][0:3, :]).then_inc(s_aggc, 1)

                def spread_of(g, u, n):
                    act.wait_ge(s_mv, 4 * g + 4)
                    nc.scalar.activation(std[:, u], mv[:, u, :, 1], ACT.Sqrt, bias=eps[:]).then_inc(s_std, 1)

                def normalise(g, u, n):
                    act.wait_ge(s_rstd, 2 * g + 2)
                    at_least(act, s_st[u], 16 * n)
                    for j in range(4):
                        nc.scalar.activation(y[:, u, j], h[:, u, j], ACT.Identity, bias=shift[:, u, j:j + 1],
                                             scale=rstd[:, u, j:j + 1]).then_inc(s_y, 1)

                rounds(act, [(keep_sums, 0), (spread_of, 2), (normalise, 3)])


_INS = ['x', 'src', 'dst', 'L0_gnn_W', 'L0_gnn_b', 'L0_gnn_agg_weight']


def kernel(**inputs):
    import numpy as _np
    import concourse.bacc as _bacc
    from concourse import mybir as _mybir
    from concourse.bass_utils import run_bass_kernel_spmd as _run

    nc = _bacc.Bacc("TRN2", target_bir_lowering=False, num_devices=1)
    arrays, args = {}, []
    for name in _INS:
        a = _np.ascontiguousarray(inputs[name])
        arrays[f"in_{name}"] = a
        args.append(nc.dram_tensor(f"in_{name}", a.shape, _mybir.dt.from_np(a.dtype), kind="ExternalInput").ap())
    slots = 4 * 128 * 128
    args.append(nc.dram_tensor("hi_scratch", (slots,), _mybir.dt.bfloat16, kind="Internal").ap())
    args.append(nc.dram_tensor("out_0", inputs['x'].shape, _mybir.dt.float32, kind="ExternalOutput").ap())
    gnn_resnorm_kernel(nc, *args)
    r = _run(nc, [arrays], core_ids=[0])
    return r.results[0]["out_0"]
```
